# Optimizing a Trainium2 kernel written in Bass

```python
import numpy as np
import jax
import jax.numpy as jnp

def _softmax(x, axis=-1):
    return jax.nn.softmax(x, axis=axis)

def _gelu(x):
    return jax.nn.gelu(x, approximate=True)

def _silu(x):
    return jax.nn.silu(x)

def _sigmoid(x):
    return jax.nn.sigmoid(x)

def _layernorm(x, axis=-1, eps=1e-05):
    m = jnp.mean(x, axis=axis, keepdims=True)
    v = jnp.var(x, axis=axis, keepdims=True)
    return (x - m) / jnp.sqrt(v + eps)

def _scatter_add(tgt, idx, src, axis=0):
    return tgt.at[idx].add(src)

def _segment_sum(src, seg, n):
    return jax.ops.segment_sum(src, seg, n)
kernel_name = 'mk_adaln_d1_jaxref_r2_8c51b6'

def setup_inputs(seed: int=0):
    np.random.seed(seed)
    _w = jnp.asarray

    def _L0_attn_setup():
        import jax, jax.numpy as jnp
        import numpy as np
        B_, S_, D_, N_ = (4, 1024, 512, 16)

        def _layernorm(y, w, b, eps=1e-05):
            mu = jnp.mean(y, axis=-1, keepdims=True)
            var = jnp.mean((y - mu) ** 2, axis=-1, keepdims=True)
            return (y - mu) * jax.lax.rsqrt(var + eps) * w + b
        key = jax.random.key(seed)
        ks = jax.random.split(key, 8)
        x = jax.random.normal(ks[0], (B_, S_, D_), dtype=jnp.float32)
        A = jax.random.normal(ks[1], (D_, N_, N_), dtype=jnp.float32) * 0.1
        Bm = jax.random.normal(ks[2], (D_, N_), dtype=jnp.float32) * 0.1
        Cm = jax.random.normal(ks[3], (D_, N_), dtype=jnp.float32) * 0.1
        Dm = jax.random.normal(ks[4], (D_,), dtype=jnp.float32) * 0.1
        ln_w = jnp.ones((D_,), dtype=jnp.float32)
        ln_b = jnp.zeros((D_,), dtype=jnp.float32)
        W_out = jax.random.normal(ks[5], (D_, D_), dtype=jnp.float32) * (1.0 / np.sqrt(D_))
        b_out = jnp.zeros((D_,), dtype=jnp.float32)
        return {'x': x, 'A': A, 'Bm': Bm, 'Cm': Cm, 'Dm': Dm, 'ln_w': ln_w, 'ln_b': ln_b, 'W_out': W_out, 'b_out': b_out}
    _L0_attn_in = _L0_attn_setup()

    def _L0_ffn_setup():
        import jax, jax.numpy as jnp
        import numpy as np
        D_MODEL = 512
        M = 64
        INNER = 16
        key = jax.random.key(seed)
        ks = jax.random.split(key, 9)

        def init(k, shape, fan_in):
            bound = 1.0 / np.sqrt(fan_in)
            return jax.random.uniform(k, shape, jnp.float32, -bound, bound)
        x = jax.random.normal(ks[0], (16, 2048, D_MODEL), dtype=jnp.float32)
        Win = init(ks[1], (D_MODEL, M), D_MODEL)
        bin_ = init(ks[2], (M,), D_MODEL)
        W1 = init(ks[3], (M, INNER), 1)
        b1 = init(ks[4], (M, INNER), 1)
        W2 = init(ks[5], (M, INNER), INNER)
        b2 = init(ks[6], (M,), INNER)
        Wout = init(ks[7], (M, D_MODEL), M)
        bout = init(ks[8], (D_MODEL,), M)
        return {'x': x, 'Win': Win, 'bin_': bin_, 'W1': W1, 'b1': b1, 'W2': W2, 'b2': b2, 'Wout': Wout, 'bout': bout}
    _L0_ffn_in = _L0_ffn_setup()
    _L0_c = _w((lambda *s: np.random.randn(*s).astype(np.float32) * 0.05)(1, 512))
    _L0_wmod = _w((lambda *s: np.random.randn(*s).astype(np.float32) * 0.05)(512, 6 * 512) * 512 ** (-0.5))
    _d = {'L0_attn_x': _L0_attn_in['x'], 'L0_attn_A': _L0_attn_in['A'], 'L0_attn_Bm': _L0_attn_in['Bm'], 'L0_attn_Cm': _L0_attn_in['Cm'], 'L0_attn_Dm': _L0_attn_in['Dm'], 'L0_attn_ln_w': _L0_attn_in['ln_w'], 'L0_attn_ln_b': _L0_attn_in['ln_b'], 'L0_attn_W_out': _L0_attn_in['W_out'], 'L0_attn_b_out': _L0_attn_in['b_out'], 'L0_ffn_Win': _L0_ffn_in['Win'], 'L0_ffn_bin_': _L0_ffn_in['bin_'], 'L0_ffn_W1': _L0_ffn_in['W1'], 'L0_ffn_b1': _L0_ffn_in['b1'], 'L0_ffn_W2': _L0_ffn_in['W2'], 'L0_ffn_b2': _L0_ffn_in['b2'], 'L0_ffn_Wout': _L0_ffn_in['Wout'], 'L0_ffn_bout': _L0_ffn_in['bout'], 'L0_c': _L0_c, 'L0_wmod': _L0_wmod}
    _x0 = _d['L0_attn_x']
    _d['L0_attn_x'] = jax.random.normal(jax.random.fold_in(jax.random.key(seed), 1), (1, 8192, 512), dtype=_x0.dtype)
    del _x0
    return _d

def reference(L0_attn_x, L0_attn_A, L0_attn_Bm, L0_attn_Cm, L0_attn_Dm, L0_attn_ln_w, L0_attn_ln_b, L0_attn_W_out, L0_attn_b_out, L0_ffn_Win, L0_ffn_bin_, L0_ffn_W1, L0_ffn_b1, L0_ffn_W2, L0_ffn_b2, L0_ffn_Wout, L0_ffn_bout, L0_c, L0_wmod):

    def _L0_attn_ref(x, A, Bm, Cm, Dm, ln_w, ln_b, W_out, b_out):
        import jax, jax.numpy as jnp
        import numpy as np
        B_, S_, D_, N_ = (4, 1024, 512, 16)

        def _layernorm(y, w, b, eps=1e-05):
            mu = jnp.mean(y, axis=-1, keepdims=True)
            var = jnp.mean((y - mu) ** 2, axis=-1, keepdims=True)
            return (y - mu) * jax.lax.rsqrt(var + eps) * w + b
        bsz = x.shape[0]
        h0 = jnp.zeros((bsz, A.shape[0], A.shape[1]), dtype=x.dtype)

        def step(h, x_t):
            h = jnp.einsum('dnm,bdm->bdn', A, h) + Bm[None] * x_t[..., None]
            y_t = jnp.einsum('dn,bdn->bd', Cm, h) + Dm * x_t
            return (h, y_t)
        _, y = jax.lax.scan(step, h0, jnp.swapaxes(x, 0, 1))
        y = jnp.swapaxes(y, 0, 1)
        y = _layernorm(y, ln_w, ln_b)
        y = jax.nn.gelu(y, approximate=False)
        y = y @ W_out.T + b_out
        return x + y

    def _L0_ffn_ref(x, Win, bin_, W1, b1, W2, b2, Wout, bout):
        import jax, jax.numpy as jnp
        import numpy as np
        D_MODEL = 512
        M = 64
        INNER = 16
        s = jnp.einsum('btd,dm->btm', x, Win) + bin_
        h = jax.nn.relu(s[..., None] * W1 + b1)
        g = jnp.einsum('btmh,mh->btm', h, W2) + b2
        out = jnp.einsum('btm,md->btd', g, Wout) + bout
        return out
    x = L0_attn_x
    mod = (_silu(L0_c) @ L0_wmod).reshape(L0_c.shape[0], 6, 1, -1)
    sa, ca, ga, sb, cb, gb = (mod[:, 0], mod[:, 1], mod[:, 2], mod[:, 3], mod[:, 4], mod[:, 5])
    ga = (2 * (ga >= 0) - 1) * jnp.maximum(jnp.abs(ga), 0.25)
    gb = (2 * (gb >= 0) - 1) * jnp.maximum(jnp.abs(gb), 0.25)
    h = _layernorm(x, axis=-1) * (1 + ca) + sa
    x = x + ga * _L0_attn_ref(h, L0_attn_A, L0_attn_Bm, L0_attn_Cm, L0_attn_Dm, L0_attn_ln_w, L0_attn_ln_b, L0_attn_W_out, L0_attn_b_out)
    h = _layernorm(x, axis=-1) * (1 + cb) + sb
    x = x + gb * _L0_ffn_ref(h, L0_ffn_Win, L0_ffn_bin_, L0_ffn_W1, L0_ffn_b1, L0_ffn_W2, L0_ffn_b2, L0_ffn_Wout, L0_ffn_bout)
    return x

_drawn_inputs = setup_inputs


def setup_inputs(seed=0):
    import zlib

    import numpy as np

    out = dict(_drawn_inputs(seed))
    spreads = {'L0_attn_ln_w': (1.0, 0.2), 'L0_attn_ln_b': (0.0, 0.518), 'L0_attn_b_out': (0.0, 0.36)}
    factors = {'L0_ffn_Win': 3.637, 'L0_ffn_bin_': 8.0, 'L0_ffn_W1': 3.605, 'L0_ffn_bout': 3.42}
    for name, (base, spread) in spreads.items():
        noise = np.random.default_rng([zlib.crc32(name.encode()), seed]).standard_normal(out[name].shape)
        drawn = base * np.exp(spread * noise) if base else spread * noise
        out[name] = jnp.asarray(drawn.astype(out[name].dtype))
    for name, factor in factors.items():
        out[name] = (out[name] * factor).astype(out[name].dtype)
    return out
```

```python
import numpy as np
import concourse.bass as bass
from concourse import mybir
from contextlib import ExitStack


P = 128
D = 512
T = 8192
NS = 16
L = P
NC = T // L
GC = P // NS
NG = D // GC
HALVES = 2
HG = NG // HALVES
HD = D // HALVES
OCT = HG // 8
LEVELS = 7
PW = L
H0 = L - NC
SCANS = 6
STEPS = LEVELS * OCT
SSTEPS = SCANS * OCT
HSTEPS = STEPS + SSTEPS
QB = D // P
M = 64
INNER = 16
EPS = 1e-5
TPS = 4
NT = NC // TPS
RELU_RING = 4


def adaln_ssm_kernel(nc, x_in, A_in, Bm_in, Cm_in, Dm_in, lnw_in, lnb_in, Wo_in, bo_in,
                     Win_in, bin_in, W1_in, b1_in, W2_in, b2_in, Wout_in, bout_in, c_in, wmod_in, out):
    f32 = mybir.dt.float32
    bf16 = mybir.dt.bfloat16
    ALU = mybir.AluOpType
    ACT = mybir.ActivationFunctionType
    AX = mybir.AxisListType

    kscr = nc.dram_tensor("kernel_taps", [D, 2 * L], f32, kind="Internal").ap()
    x_t = x_in[0].rearrange("(c p) d -> p c d", p=P)
    out_t = out[0].rearrange("(c p) d -> p c d", p=P)

    ctx = ExitStack()
    with ctx:
        def sb(name, shape, dt=f32):
            return ctx.enter_context(nc.sbuf_tensor(name, shape, dt))

        def sem(name):
            return ctx.enter_context(nc.semaphore(name))

        XY = sb("XY", [P, D, NC])
        A0 = sb("arenaA", [P, 8736])
        PV = A0[:, 0:HG * 144].rearrange("p (g w) -> p g w", w=144)
        WP = A0[:, 4608:4608 + HG * 129].rearrange("p (g w) -> p g w", w=129)
        BDa = sb("BDa", [P, 2, 8, P])
        BDTa = sb("BDTa", [P, 2, 8, P])
        B0 = sb("arenaB", [P, 4096])
        UR = B0[:, 0:1024]
        TRr = B0[:, 1024:4096]
        ROWS = sb("ROWS", [P, 4, D])
        ident = sb("ident", [P, P])
        bcs = sb("bcs", [P, 256])
        mask8 = sb("mask8", [P, GC])
        par = sb("par", [P, 2])
        ST = sb("ST", [P, 3, NC])
        ccol = sb("ccol", [P, QB])
        DmT = sb("DmT", [P, QB])
        cbsb = sb("cbsb", [P, 2 * QB])
        lnwb = sb("lnwb", [P, 2 * QB])
        bs6 = sb("bs6", [P, 4, 6])
        half_neg = sb("half_neg", [P, 8])

        CA1, SA, GA, GB = (ROWS[:, i, :] for i in range(4))
        mean_x, rstd_x, nmr_x = (ST[:, i, :] for i in range(3))
        wm = XY[:, 0:6 * 4 * 8, :].rearrange("p (j k r) c -> p j k (r c)", j=6, k=4)
        crep = XY[:, 192:200, :].rearrange("p (k r) c -> p k (r c)", k=4)
        cbrow = UR[:, 0:512]
        sbrow = UR[:, 512:1024]
        bcn = bcs[:, 0:128]
        BCT = bcs[:, 128:256]
        CM = UR[:, 0:256].rearrange("p (g c) -> p g c", c=GC)
        ksb = UR[:, 256:512]
        ktz = UR[:, 512:1024].rearrange("p (b w) -> p b w", b=2)
        Uring = UR.rearrange("p (r w) -> p r w", r=2)
        BDH = UR.rearrange("p (r h c) -> p r h c", r=2, h=GC)
        Tring = TRr.rearrange("p (r h i) -> p r h i", r=3, h=GC)
        xst = TRr[:, 0:1536].rearrange("p (r d) -> p r d", r=3)
        xhs = TRr[:, 1536:3072].rearrange("p (r d) -> p r d", r=3)
        zT = A0[:, 0:4096].rearrange("p (r q t) -> p r q t", r=2, q=QB)
        hatX = A0[:, 4096:6144].rearrange("p (t d) -> p t d", t=TPS)
        x2T = A0[:, 6144:7168].rearrange("p (r t) -> p r t", r=2)
        WinS = A0[:, 7168:7424].rearrange("p (q m) -> p q m", q=QB)
        WoutS = A0[:, 7424:8448].rearrange("p (r d) -> p r d", r=2)
        bias2 = A0[:, 8448:8704].bitcast(bf16)
        hatY = BDa[:, 0:2, :, :].rearrange("p r g j -> p (r g j)").rearrange("p (t d) -> p t d", t=TPS)
        WoN = BDa[:, :, :, :].rearrange("p r g j -> p (r g j)").rearrange("p (o d) -> p o d", o=QB)
        WoT = BDTa[:, :, :, :].rearrange("p r g j -> p (r g j)").rearrange("p (q d) -> p q d", q=QB)
        xr = B0[:, :].rearrange("p (r t d) -> p r t d", r=2, t=TPS)
        Grow = CA1
        tmp = SA
        rr = ROWS[:, 2:4, :].rearrange("p a (b t) -> p (a b) t", b=2)
        gS = sb("gS", [P, 256])
        bias1 = sb("bias1", [P, D], bf16)
        ones_bf = sb("ones_bf", [P, P], bf16)
        sS = bcs[:, 0:256]
        ffc = sb("ffc", [P, 3 * INNER + 4])
        W1c, b1c, W2c = (ffc[:, i * INNER:(i + 1) * INNER] for i in range(3))
        b2c, binc = ffc[:, 48:49], ffc[:, 49:50]
        mvy = sb("mvy", [P, TPS, 2])
        mvx = sb("mvx", [P, TPS, 2])
        sy = sb("sy", [P, 2, TPS])
        s2 = sb("s2", [P, 2, TPS])
        sx = sb("sx", [P, 2, 2, TPS])

        PS = ctx.enter_context(nc.psum_tensor("PS", [P, 8, 512], f32))

        def pv_ps(r):
            return PS[:, 2 * r:2 * r + 2, :].rearrange("p b (s w) -> p (b s) w", w=128)

        def w_ps(r):
            return PS[:, 4 + r, :].rearrange("p (g w) -> p g w", w=64)

        S = {}
        for name in ("consts", "ident_r", "ld_c", "ld_bc", "ld_A", "ld_small", "silu_r", "crep_r", "mod_mm", "mod_ev", "cb_mm",
                     "cb_ev", "bct_mm", "bct_ev", "par_r", "v0_r", "w0_r",
                     "bn_r", "rst_r", "xh_r", "xm_r", "xy_r", "dchain", "pchain",
                     "bd_r", "bdt_r", "lvl_mm", "lvl_ev", "scan_h", "cm_r", "kz_r", "k_mm", "k_sb", "kt_mm", "kt_r", "k_saved",
                     "ut_mm", "ut_ev", "u_mm", "u_ev", "bdh_r", "o_mm", "t_mm", "y_ev", "bz_r",
                     "ld_wo", "wo_tr", "wo_ev", "ld_w", "prep_r", "b2_mm", "prep_p", "prep_mm",
                     "ty_mm", "gelu_r", "o1_mm", "x2_r", "yst", "yr_r", "yh_r", "x2st", "x2rs", "xh2_r", "tx_mm", "xT_r",
                     "s_mm", "s_ev", "st_mm", "relu_r", "ffn_r", "o2_mm", "x3_r", "sx_r", "xres_r"):
            S[name] = sem(name)
        ld_wm = [sem(f"ld_wm{j}") for j in range(6)]
        x_ld = [sem(f"x_ld{r}") for r in range(3)]
        t_ld = [sem(f"t_ld{r}") for r in range(3)]
        xc_ld = [sem(f"xc_ld{r}") for r in range(2)]
        x_st = [sem(f"x_st{r}") for r in range(2)]

        MOD_ORDER = [1, 0, 2, 5, 4, 3]

        def tiles_of(n):
            return range(NC * n // STEPS, NC * (n + 1) // STEPS)

        block = ctx.enter_context(nc.Block())

        @block.sync
        def _(sp):
            with nc.allow_non_contiguous_dma(reason="columns of a few hundred elements"):
                sp.dma_start(ccol[:, :], c_in[0].rearrange("(k p) -> p k", p=P)).then_inc(S["ld_c"], 16)
                sp.dma_start(bcn[0:64, :], Bm_in.rearrange("(g c) n -> g (c n)", c=GC)).then_inc(S["ld_bc"], 16)
                sp.dma_start(bcn[64:128, :], Cm_in.rearrange("(g c) n -> g (c n)", c=GC)).then_inc(S["ld_bc"], 16)
                wv = wmod_in.rearrange("(k p) n -> p k n", p=P)
                for i in range(2):
                    j = MOD_ORDER[i]
                    sp.dma_start(wm[:, j, :, :], wv[:, :, j * D:(j + 1) * D]).then_inc(ld_wm[j], 16)
            Av = A_in.rearrange("(g c) n m -> (c n) g m", c=GC)

            def load_A(half):
                sp.dma_start(PV[:, :, PW:PW + NS], Av[:, half * HG:(half + 1) * HG, :]).then_inc(S["ld_A"], 16)

            load_A(0)
            with nc.allow_non_contiguous_dma(reason="columns of a few hundred elements"):
                sp.dma_start(DmT[:, :], Dm_in.rearrange("(k p) -> p k", p=P)).then_inc(S["ld_small"], 16)
                sp.dma_start(lnwb[:, 0:QB], lnw_in.rearrange("(k p) -> p k", p=P)).then_inc(S["ld_small"], 16)
                sp.dma_start(lnwb[:, QB:], lnb_in.rearrange("(k p) -> p k", p=P)).then_inc(S["ld_small"], 16)

            def load_x(c):
                if c >= 3:
                    sp.wait_ge(S["xh_r"], c - 2)
                sp.dma_start(xst[:, c % 3, :], x_t[:, c, :]).then_inc(x_ld[c % 3], 16)

            for c in range(3):
                load_x(c)
            for i in range(2, 6):
                j = MOD_ORDER[i]
                sp.dma_start(wm[:, j, :, :], wv[:, :, j * D:(j + 1) * D]).then_inc(ld_wm[j], 16)
            for c in range(3, NC):
                load_x(c)
            for half in range(HALVES):
                if half:
                    sp.wait_ge(S["o_mm"], half * HG)
                    sp.wait_ge(S["bdh_r"], half * HG)
                    load_A(half)
                sp.wait_ge(S["kt_r"], half + 1)
                sp.dma_start(kscr[half * HD:(half + 1) * HD, :].rearrange("(b p) w -> p b w", p=P), ktz).then_inc(S["k_saved"], 16)
                sp.wait_ge(S["k_saved"], 16 * (half + 1))
                if half == 0:
                    sp.wait_ge(S["xy_r"], NC)
                for g in range(HG):
                    n = half * HG + g
                    if n >= 3:
                        sp.wait_ge(S["t_mm"], n - 2)
                    row = (half * HG + g) * GC
                    src = bass.AP(kscr.tensor, row * 2 * L, [[1, P], [2 * L, GC], [1, L]])
                    sp.dma_start(Tring[:, n % 3, :, :], src).then_inc(t_ld[n % 3], 16)
                    if half == HALVES - 1 and g == 0:
                        sp.wait_ge(S["lvl_mm"], HALVES * HSTEPS)
                        sp.dma_start(WoN, Wo_in.rearrange("(o p) d -> p o d", p=P)).then_inc(S["ld_wo"], 16)
            sp.wait_ge(S["t_mm"], NG)
            sp.wait_ge(S["bdh_r"], NG)
            with nc.allow_non_contiguous_dma(reason="columns of a few hundred elements"):
                sp.dma_start(WinS, Win_in.rearrange("(q p) m -> p q m", p=P)).then_inc(S["ld_w"], 16)
                for r in range(2):
                    sp.dma_start(WoutS[64 * r:64 * r + 64, r, :], Wout_in).then_inc(S["ld_w"], 16)
                    for dst, src in ((W1c, W1_in), (b1c, b1_in), (W2c, W2_in)):
                        sp.dma_start(dst[64 * r:64 * r + 64, :], src).then_inc(S["ld_w"], 16)
                    sp.dma_start(b2c[64 * r:64 * r + 64, :], b2_in.rearrange("(m a) -> m a", a=1)).then_inc(S["ld_w"], 16)
                    sp.dma_start(binc[64 * r:64 * r + 64, :], bin_in.rearrange("(m a) -> m a", a=1)).then_inc(S["ld_w"], 16)
                sp.dma_start(zT[:, 0, 0, :], bo_in.partition_broadcast(P)).then_inc(S["ld_w"], 16)
                sp.dma_start(zT[:, 0, 1, :], bout_in.partition_broadcast(P)).then_inc(S["ld_w"], 16)

            def load_super(s, b):
                sp.dma_start(xr[:, b, :, :], x_t[:, bass.ds(s * TPS, TPS), :]).then_inc(xc_ld[b], 16)

            def store_super(s, b):
                sp.dma_start(out_t[:, bass.ds(s * TPS, TPS), :], xr[:, b, :, :]).then_inc(x_st[b], 16)

            load_super(0, 0)
            load_super(1, 1)
            for s in range(1, NT + 1):
                b = (s - 1) % 2
                sp.wait_ge(S["x3_r"], TPS * s)
                store_super(s - 1, b)
                sp.wait_ge(x_st[b], 16 * ((s - 1) // 2 + 1))
                if s + 1 < NT:
                    load_super(s + 1, b)

        @block.gpsimd
        def _(gp):
            nch = [0]

            def chain(ins):
                nch[0] += 1
                ins.then_inc(S["pchain"], 1)
                gp.wait_ge(S["pchain"], nch[0])

            chain(gp.memset(ident[:, :], 0.0))
            gp.affine_select(out=ident[:, :], in_=ident[:, :], compare_op=ALU.not_equal, fill=1.0, base=0,
                             pattern=[[-1, P]], channel_multiplier=1).then_inc(S["ident_r"], 1)
            gp.memset(half_neg[:, :], -0.5).then_inc(S["consts"], 1)
            gp.memset(ones_bf[:, :], 1.0).then_inc(S["consts"], 1)
            chain(gp.memset(mask8[:, :], 1.0))
            chain(gp.affine_select(out=mask8[:, :], in_=mask8[:, :], compare_op=ALU.is_ge, fill=0.0, base=0,
                                   pattern=[[-NS, GC]], channel_multiplier=1))
            gp.affine_select(out=mask8[:, :], in_=mask8[:, :], compare_op=ALU.is_ge, fill=0.0, base=NS - 1,
                             pattern=[[NS, GC]], channel_multiplier=-1).then_inc(S["consts"], 1)
            gp.wait_ge(S["consts"], 3)

            def block_diag(half, k, o, n):
                if k == 0:
                    if o == 0:
                        gp.wait_ge(S["ld_A"], 16 * (half + 1))
                else:
                    gp.wait_ge(S["lvl_ev"], n - OCT + 1)
                if n >= 2:
                    gp.wait_ge(S["lvl_mm"], n - 1)
                src = PV[:, 8 * o:8 * o + 8, PW:PW + NS].unsqueeze(2).to_broadcast([P, 8, GC, NS])
                msk = mask8[:, :].unsqueeze(1).unsqueeze(3).to_broadcast([P, 8, GC, NS])
                gp.tensor_tensor(BDa[:, n % 2, :, :].rearrange("p g (c m) -> p g c m", m=NS), src, msk,
                                 ALU.mult).then_inc(S["bd_r"], 1)

            def rstd_of(var, mean, rstd, nmr, w, done):
                chain(gp.tensor_scalar(rstd, var, EPS, 0.0, ALU.add, ALU.add))
                chain(gp.tensor_tensor(rstd, rstd, half_neg[:, 0:w], ALU.pow))
                chain(gp.tensor_tensor(nmr, mean, rstd, ALU.mult))
                gp.tensor_scalar(nmr, nmr, -1.0, 0.0, ALU.mult, ALU.add).then_inc(done, 1)

            def scale_x(c):
                gp.wait_ge(S["xh_r"], c + 1)
                if c == 0:
                    gp.wait_ge(S["mod_ev"], 1)
                gp.tensor_tensor(xhs[:, c % 3, :], xhs[:, c % 3, :], CA1, ALU.mult).then_inc(S["xm_r"], 1)

            for half in range(HALVES):
                base = half * HSTEPS
                for n in range(STEPS):
                    block_diag(half, n // OCT, n % OCT, base + n)
                    if half == 0:
                        for c in tiles_of(n):
                            gp.wait_ge(S["bn_r"], c + 1)
                            rstd_of(rstd_x[:, c:c + 1], mean_x[:, c:c + 1], rstd_x[:, c:c + 1], nmr_x[:, c:c + 1], 1, S["rst_r"])
                            if c >= 1:
                                scale_x(c - 1)
                    if n == 1:
                        if half == 0:
                            gp.wait_ge(S["cb_mm"], 1)
                            gp.wait_ge(S["bct_ev"], 1)
                        else:
                            gp.wait_ge(S["o_mm"], half * HG)
                        cb = BCT[:, 64 + half * HG:64 + (half + 1) * HG].unsqueeze(2).to_broadcast([P, HG, GC])
                        gp.tensor_tensor(CM, cb, mask8[:, :].unsqueeze(1).to_broadcast([P, HG, GC]), ALU.mult).then_inc(S["cm_r"], 1)
                        gp.memset(ktz, 0.0).then_inc(S["kz_r"], 1)
                if half == 0:
                    scale_x(NC - 1)
                for i in range(SSTEPS):
                    block_diag(half, LEVELS + i // OCT, i % OCT, base + STEPS + i)
                gp.wait_ge(S["u_mm"], 8 * (half + 1))
                gp.memset(BDH[:, :, :, 0:1], 0.0).then_inc(S["bz_r"], 1)
                for g in range(HG):
                    n = half * HG + g
                    if g % 8 == 0:
                        gp.wait_ge(S["scan_h"], half * SSTEPS + SSTEPS - OCT + g // 8 + 1)
                    if g >= 2:
                        gp.wait_ge(S["o_mm"], n - 1)
                    gp.tensor_tensor(BDH[:, g % 2, :, 1:NC], PV[:, g, H0:H0 + NC - 1].unsqueeze(1).to_broadcast([P, GC, NC - 1]),
                                     mask8[:, :].unsqueeze(2).to_broadcast([P, GC, NC - 1]), ALU.mult).then_inc(S["bdh_r"], 1)

            gp.wait_ge(S["t_mm"], NG)
            gp.wait_ge(S["bdh_r"], NG)
            gp.memset(WoutS[64:128, 0, :], 0.0).then_inc(S["prep_p"], 1)
            gp.memset(WoutS[0:64, 1, :], 0.0).then_inc(S["prep_p"], 1)
            gp.wait_ge(S["prep_p"], 2)

            def rstd_y(s):
                gp.wait_ge(S["yst"], s + 1)
                if s >= 1:
                    gp.wait_ge(S["yh_r"], TPS * s)
                rstd_of(mvy[:, :, 1], mvy[:, :, 0], sy[:, 0, :], sy[:, 1, :], TPS, S["yr_r"])

            def residual(s):
                b = s % 2
                gp.wait_ge(xc_ld[b], 16 * (s // 2 + 1))
                gp.wait_ge(S["sx_r"], s + 1)
                for t in range(TPS):
                    chain(gp.tensor_scalar(tmp, xr[:, b, t, :], sx[:, b, 0, t:t + 1], sx[:, b, 1, t:t + 1], ALU.mult, ALU.add))
                    chain(gp.tensor_tensor(tmp, tmp, Grow, ALU.mult))
                    ins = gp.tensor_tensor(xr[:, b, t, :], xr[:, b, t, :], tmp, ALU.add)
                    ins.then_inc(S["xres_r"], 1)
                    gp.wait_ge(S["xres_r"], TPS * s + t + 1)

            rstd_y(0)
            gp.wait_ge(S["prep_r"], 2)
            residual(0)
            rstd_y(1)
            for s in range(NT):
                gp.wait_ge(S["x2st"], s + 1)
                if s >= 1:
                    gp.wait_ge(S["xh2_r"], TPS * s)
                rstd_of(mvx[:, :, 1], mvx[:, :, 0], s2[:, 0, :], s2[:, 1, :], TPS, S["x2rs"])
                if s + 2 < NT:
                    rstd_y(s + 2)
                if s + 1 < NT:
                    residual(s + 1)

        @block.scalar
        def _(act):
            act.wait_ge(S["ld_c"], 16)
            act.activation(ccol[:, :], ccol[:, :], ACT.Silu).then_inc(S["silu_r"], 1)
            act.wait_ge(S["bct_mm"], 1)
            act.activation(BCT, PS[:, 7, 0:128], ACT.Copy).then_inc(S["bct_ev"], 1)
            act.wait_ge(S["bct_ev"], 1)

            def normalise_x(c):
                act.wait_ge(S["rst_r"], c + 1)
                if c >= 3:
                    act.wait_ge(S["xy_r"], c - 2)
                act.activation(xhs[:, c % 3, :], xst[:, c % 3, :], ACT.Identity, scale=rstd_x[:, c:c + 1],
                               bias=nmr_x[:, c:c + 1]).then_inc(S["xh_r"], 1)

            for half in range(HALVES):
                base = half * HSTEPS
                if half:
                    act.wait_ge(S["o_mm"], half * HG)
                    act.wait_ge(S["bdh_r"], half * HG)
                act.activation(PV[:, :, PW - 1], BCT[:, half * HG:(half + 1) * HG], ACT.Copy).then_inc(S["v0_r"], 1)
                act.activation(WP[:, :, L], BCT[:, 64 + half * HG:64 + (half + 1) * HG], ACT.Copy).then_inc(S["v0_r"], 1)
                for n in range(STEPS):
                    if half == 0:
                        for c in tiles_of(n):
                            normalise_x(c)
                    k, o, r, w = n // OCT, n % OCT, (base + n) % 2, 2 ** (n // OCT)
                    act.wait_ge(S["lvl_mm"], base + n + 1)
                    act.activation(PV[:, 8 * o:8 * o + 8, PW:PW + NS], pv_ps(r)[:, :, w:w + NS], ACT.Copy)
                    act.activation(PV[:, 8 * o:8 * o + 8, PW - 2 * w:PW - w], pv_ps(r)[:, :, 0:w], ACT.Copy)
                    act.activation(WP[:, 8 * o:8 * o + 8, L + 1 - 2 * w:L + 1 - w], w_ps(r)[:, :, 0:w], ACT.Copy).then_inc(S["lvl_ev"], 1)
                for q in range(8):
                    n = 8 * half + q
                    act.wait_ge(S["ut_mm"], n + 1)
                    if q == 0:
                        act.wait_ge(S["k_saved"], 16 * (half + 1))
                    if q >= 2:
                        act.wait_ge(S["u_mm"], n - 1)
                    act.activation(Uring[:, q % 2, :], PS[:, 6 + q % 2, :], ACT.Copy).then_inc(S["ut_ev"], 1)
                for i in range(SSTEPS):
                    k, o, n = i // OCT, i % OCT, base + STEPS + i
                    r = n % 2
                    act.wait_ge(S["lvl_mm"], n + 1)
                    if k == 0:
                        act.activation(WP[:, 8 * o:8 * o + 8, 0], w_ps(r)[:, :, 0], ACT.Copy)
                    act.activation(PV[:, 8 * o:8 * o + 8, PW:PW + NS], pv_ps(r)[:, :, NC:NC + NS], ACT.Copy).then_inc(S["lvl_ev"], 1)
                for g in range(HG):
                    n = half * HG + g
                    act.wait_ge(S["t_mm"], n + 1)
                    d = n * GC
                    act.activation(XY[:, d:d + GC, :], PS[:, g % 4, :].rearrange("p (h c) -> p h c", h=GC),
                                   ACT.Copy).then_inc(S["y_ev"], 1)

            def yhat(s):
                act.wait_ge(S["yr_r"], s + 1)
                if s >= 1:
                    act.wait_ge(S["ty_mm"], TPS * s)
                else:
                    act.wait_ge(S["wo_tr"], QB)
                for t in range(TPS):
                    act.activation(hatY[:, t, :], XY[:, :, s * TPS + t], ACT.Identity, scale=sy[:, 0, t:t + 1],
                                   bias=sy[:, 1, t:t + 1]).then_inc(S["yh_r"], 1)

            def gelu(s):
                if s >= 2:
                    act.wait_ge(S["o1_mm"], TPS * (s - 1))
                if s == 0:
                    act.wait_ge(S["prep_r"], 2)
                for q in range(QB):
                    act.wait_ge(S["ty_mm"], QB * s + q + 1)
                    act.activation(zT[:, s % 2, q, :].rearrange("p (t i) -> p t i", i=P),
                                   PS[:, q % 2, :].rearrange("p (t i) -> p t i", i=P)[:, :, ::-1], ACT.Gelu, scale=lnwb[:, q:q + 1],
                                   bias=lnwb[:, QB + q:QB + q + 1]).then_inc(S["gelu_r"], 1)

            def relus(s):
                act.wait_ge(S["st_mm"], s + 1)
                for h in range(INNER):
                    n = INNER * s + h
                    if n >= RELU_RING:
                        act.wait_ge(S["ffn_r"], n - RELU_RING + 1)
                    act.activation(rr[:, h % RELU_RING, :], PS[:, 5, 0:256], ACT.Relu, scale=W1c[:, h:h + 1],
                                   bias=b1c[:, h:h + 1]).then_inc(S["relu_r"], 1)

            act.wait_ge(S["ld_small"], 48)
            yhat(0)
            gelu(0)
            yhat(1)
            for s in range(NT + 1):
                if s >= 1:
                    relus(s - 1)
                if s == NT:
                    break
                if s + 1 < NT:
                    gelu(s + 1)
                act.wait_ge(S["x2rs"], s + 1)
                if s >= 1:
                    act.wait_ge(S["tx_mm"], QB * s)
                for t in range(TPS):
                    act.activation(hatX[:, t, :], xr[:, s % 2, t, :], ACT.Identity, scale=s2[:, 0, t:t + 1],
                                   bias=s2[:, 1, t:t + 1]).then_inc(S["xh2_r"], 1)
                for q in range(QB):
                    n = QB * s + q
                    act.wait_ge(S["tx_mm"], n + 1)
                    if n >= 2:
                        act.wait_ge(S["s_mm"], n - 1)
                    act.activation(x2T[:, q % 2, :], PS[:, q % 2, :], ACT.Copy).then_inc(S["xT_r"], 1)
                if s + 2 < NT:
                    yhat(s + 2)

        @block.vector
        def _(dve):
            nch = [0]

            def chain(ins):
                nch[0] += 1
                ins.then_inc(S["dchain"], 1)
                dve.wait_ge(S["dchain"], nch[0])

            dve.wait_ge(S["silu_r"], 1)
            dve.tensor_copy(crep, ccol[:, :].unsqueeze(2).to_broadcast([P, QB, P])).then_inc(S["crep_r"], 1)
            dve.wait_ge(S["consts"], 3)
            for e in range(2):
                dve.reduce_sum(par[:, e:e + 1], mask8[:, e::2], AX.X).then_inc(S["par_r"], 1)

            def mod_rows():
                for i, j in enumerate(MOD_ORDER):
                    dve.wait_ge(S["mod_mm"], i + 1)
                    src = PS[:, i, :]
                    if j == 1:
                        dve.tensor_scalar(CA1, src, 1.0, None, ALU.add).then_inc(S["mod_ev"], 1)
                    elif j == 0:
                        dve.tensor_copy(SA, src).then_inc(S["mod_ev"], 1)
                    elif j in (2, 5):
                        row = GA if j == 2 else GB
                        dve.tensor_scalar(cbrow, src, 0.0, 2.0, ALU.is_ge, ALU.mult)
                        chain(dve.tensor_scalar(row, src, -1.0, 0.25, ALU.mult, ALU.max))
                        chain(dve.tensor_tensor(row, row, src, ALU.max))
                        ins = dve.scalar_tensor_tensor(out=row, in0=cbrow, scalar=-1.0, in1=row, op0=ALU.add, op1=ALU.mult)
                        ins.then_inc(S["mod_ev"], 1)
                        dve.wait_ge(S["mod_ev"], i + 1)
                    elif j == 4:
                        dve.tensor_scalar(cbrow, src, 1.0, None, ALU.add).then_inc(S["mod_ev"], 1)
                    else:
                        dve.tensor_copy(sbrow, src).then_inc(S["mod_ev"], 1)
                dve.wait_ge(S["cb_mm"], 1)
                dve.tensor_copy(cbsb[:, :], PS[:, 6, 0:8]).then_inc(S["cb_ev"], 1)

            def stats_x(c):
                dve.wait_ge(x_ld[c % 3], 16 * (c // 3 + 1))
                if c >= 4:
                    dve.wait_ge(S["bn_r"], c - 3)
                chain(dve.bn_stats(bs6[:, c % 4, :], xst[:, c % 3, :]))
                dve.bn_aggr(ST[:, 0:2, c], bs6[:, c % 4, :]).then_inc(S["bn_r"], 1)

            def shift_x(c):
                dve.wait_ge(S["xm_r"], c + 1)
                dve.tensor_tensor(XY[:, :, c], xhs[:, c % 3, :], SA, ALU.add).then_inc(S["xy_r"], 1)

            def transpose_bd(n):
                dve.wait_ge(S["bd_r"], n + 1)
                dve.transpose(BDTa[:, n % 2, :, :], BDa[:, n % 2, :, :]).then_inc(S["bdt_r"], 1)

            for half in range(HALVES):
                base = half * HSTEPS
                for n in range(STEPS):
                    if n == 0 and half == 0:
                        for c in tiles_of(0):
                            stats_x(c)
                        mod_rows()
                        transpose_bd(0)
                        continue
                    if half == 0:
                        for c in tiles_of(n):
                            stats_x(c)
                            shift_x(c - 2)
                    transpose_bd(base + n)
                if half == 0:
                    for c in (NC - 2, NC - 1):
                        shift_x(c)
                dve.wait_ge(S["k_mm"], half + 1)
                dve.tensor_copy(ksb, PS[:, 6, 0:HD]).then_inc(S["k_sb"], 1)
                dve.wait_ge(S["kt_mm"], half + 1)
                dve.wait_ge(S["kz_r"], half + 1)
                if half == 0:
                    dve.wait_ge(S["ld_small"], 48)
                chain(dve.tensor_copy(ktz[:, :, 0:L], PS[:, 7, 0:HD].rearrange("p (b w) -> p b w", b=2)))
                dve.tensor_tensor(ktz[:, :, L - 1], ktz[:, :, L - 1], DmT[:, 2 * half:2 * half + 2], ALU.add).then_inc(S["kt_r"], 1)
                if half == 0:
                    dve.wait_ge(S["par_r"], 2)
                for q in range(8):
                    n = 8 * half + q
                    dve.wait_ge(S["u_mm"], n + 1)
                    ps = PS[:, q % 4, :].rearrange("p (g a c) -> p g a c", g=4, a=2)
                    st = PV[:, 4 * q:4 * q + 4, H0:H0 + NC]
                    chain(dve.tensor_scalar(st, ps[:, :, 0, :], par[:, 0:1], None, ALU.mult))
                    dve.scalar_tensor_tensor(out=st, in0=ps[:, :, 1, :], scalar=par[:, 1:2], in1=st, op0=ALU.mult,
                                             op1=ALU.add).then_inc(S["u_ev"], 1)
                dve.wait_ge(S["u_ev"], 8 * (half + 1))
                for i in range(SSTEPS):
                    k, o, n = i // OCT, i % OCT, base + STEPS + i
                    transpose_bd(n)
                    if i >= 1:
                        scan_add(dve, S, PV, pv_ps, half, base, i - 1, ALU)
                scan_add(dve, S, PV, pv_ps, half, base, SSTEPS - 1, ALU)

            for q in range(QB):
                dve.wait_ge(S["wo_tr"], q + 1)
                dve.tensor_tensor(WoT[:, q, :], PS[:, 6 + q % 2, :], GA, ALU.mult).then_inc(S["wo_ev"], 1)

            def y_stats(s):
                if s >= 1:
                    dve.wait_ge(S["yr_r"], s)
                for t in range(TPS):
                    dve.bn_stats(bs6[:, t, :], XY[:, :, s * TPS + t]).then_inc(S["dchain"], 1)
                nch[0] += TPS
                dve.wait_ge(S["dchain"], nch[0])
                for t in range(TPS):
                    ins = dve.bn_aggr(mvy[:, t, :], bs6[:, t, :])
                    if t < TPS - 1:
                        ins.then_inc(S["dchain"], 1)
                nch[0] += TPS - 1
                ins.then_inc(S["yst"], 1)
                dve.wait_ge(S["yst"], s + 1)
                dve.wait_ge(S["dchain"], nch[0])

            def x_stats(s):
                if s >= 2:
                    dve.wait_ge(S["xres_r"], TPS * (s - 1))
                dve.tensor_copy(sx[:, s % 2, :, :], ST[:, 1:3, s * TPS:(s + 1) * TPS]).then_inc(S["sx_r"], 1)

            dve.wait_ge(S["y_ev"], NG)
            x_stats(0)
            y_stats(0)
            dve.wait_ge(S["ld_w"], 16 * 15)
            dve.wait_ge(S["prep_p"], 2)
            b1row, b2row = zT[:, 0, 0, :], zT[:, 0, 1, :]
            dve.wait_ge(S["prep_mm"], 1)
            dve.tensor_tensor(binc, binc, PS[:, 5, 0:1], ALU.add).then_inc(S["dchain"], 1)
            for q in range(QB):
                dve.tensor_scalar(WinS[:, q, :], WinS[:, q, :], cbsb[:, q:q + 1], None, ALU.mult).then_inc(S["dchain"], 1)
            dve.tensor_tensor(b1row, b1row, SA, ALU.add).then_inc(S["dchain"], 1)
            for r in range(2):
                dve.tensor_tensor(WoutS[:, r, :], WoutS[:, r, :], GB, ALU.mult).then_inc(S["dchain"], 1)
            dve.tensor_tensor(Grow, CA1, GA, ALU.mult).then_inc(S["dchain"], 1)
            nch[0] += 1 + QB + 1 + 2 + 1
            dve.wait_ge(S["dchain"], nch[0])
            chain(dve.scalar_tensor_tensor(out=b1c, in0=W1c, scalar=binc, in1=b1c, op0=ALU.mult, op1=ALU.add))
            chain(dve.tensor_tensor(b2row, b2row, GB, ALU.mult))
            chain(dve.tensor_tensor(b1row, b1row, GA, ALU.mult))
            rest, part, acc = zT[:, 0, 2, :], zT[:, 0, 3, :].bitcast(bf16)[:, 0:D], zT[:, 1, 0, :]
            up = zT[:, 1, 1, :]
            for row, dst in ((b1row, bias1[:, :]), (b2row, bias2)):
                chain(dve.tensor_copy(rest, row))
                for i in range(3):
                    chain(dve.tensor_copy(part, rest))
                    chain(dve.tensor_copy(up, part))
                    if i == 0:
                        chain(dve.tensor_scalar(acc, up, ident[:, i:i + 1], None, ALU.mult))
                    else:
                        chain(dve.scalar_tensor_tensor(out=acc, in0=up, scalar=ident[:, i:i + 1], in1=acc, op0=ALU.mult, op1=ALU.add))
                    chain(dve.tensor_tensor(rest, rest, up, ALU.subtract))
                ins = dve.tensor_copy(dst, acc)
                ins.then_inc(S["prep_r"], 1)
            dve.wait_ge(S["prep_r"], 2)

            def ffn(s):
                for h in range(INNER):
                    n = INNER * s + h
                    dve.wait_ge(S["relu_r"], n + 1)
                    if h == 0:
                        if s >= 1:
                            dve.wait_ge(S["o2_mm"], TPS * s)
                        ins = dve.tensor_scalar(gS[:, :], rr[:, 0, :], W2c[:, 0:1], b2c, ALU.mult, ALU.add)
                    else:
                        dve.wait_ge(S["ffn_r"], n)
                        ins = dve.scalar_tensor_tensor(out=gS[:, :], in0=rr[:, h % RELU_RING, :], scalar=W2c[:, h:h + 1],
                                                       in1=gS[:, :], op0=ALU.mult, op1=ALU.add)
                    ins.then_inc(S["ffn_r"], 1)

            x_stats(1)
            y_stats(1)
            for s in range(NT + 1):
                if s >= 1:
                    ffn(s - 1)
                if s < NT:
                    b = s % 2
                    for t in range(TPS):
                        n = TPS * s + t
                        dve.wait_ge(S["o1_mm"], n + 1)
                        dve.wait_ge(S["xres_r"], n + 1)
                        dve.tensor_tensor(xr[:, b, t, :], xr[:, b, t, :], PS[:, 2 + t % 2, :], ALU.add).then_inc(S["x2_r"], 1)
                        dve.wait_ge(S["x2_r"], n + 1)
                        chain(dve.bn_stats(bs6[:, t, :], xr[:, b, t, :]))
                    if s >= 1:
                        dve.wait_ge(S["x2rs"], s)
                    for t in range(TPS):
                        ins = dve.bn_aggr(mvx[:, t, :], bs6[:, t, :])
                    ins.then_inc(S["x2st"], 1)
                if s >= 1:
                    b = (s - 1) % 2
                    for t in range(TPS):
                        n = TPS * (s - 1) + t
                        dve.wait_ge(S["o2_mm"], n + 1)
                        if t == 0 and s < NT:
                            pass
                        dve.wait_ge(S["xh2_r"], TPS * s)
                        dve.tensor_tensor(xr[:, b, t, :], xr[:, b, t, :], PS[:, 6 + t % 2, :], ALU.add).then_inc(S["x3_r"], 1)
                if s < NT:
                    if s + 2 < NT:
                        dve.wait_ge(S["x2st"], s + 1)
                        x_stats(s + 2)
                        y_stats(s + 2)
                    dve.wait_ge(S["s_mm"], QB * (s + 1))
                    if s >= 1:
                        dve.wait_ge(S["st_mm"], s)
                    dve.tensor_copy(sS, PS[:, 4, 0:256]).then_inc(S["s_ev"], 1)

        @block.tensor
        def _(pe):
            pe.wait_ge(S["ident_r"], 1)
            pe.wait_ge(S["ld_bc"], 32)
            pe.transpose(PS[:, 7, 0:128], bcn, ident[:, :]).then_inc(S["bct_mm"], 1)
            pe.wait_ge(S["crep_r"], 1)
            for i, j in enumerate(MOD_ORDER):
                pe.wait_ge(ld_wm[j], 16)
                for k in range(QB):
                    mm = pe.matmul(PS[:, i, :], crep[:, k, :], wm[:, j, k, :], start=(k == 0), stop=(k == QB - 1))
                mm.then_inc(S["mod_mm"], 1)
            pe.wait_ge(S["mod_ev"], 6)
            for i in range(8):
                row = cbrow if i < 4 else sbrow
                mm = pe.matmul(PS[:, 6, i:i + 1], row[0:1, (i % 4) * P:(i % 4 + 1) * P], ones1(ident), start=True, stop=True)
            mm.then_inc(S["cb_mm"], 1)
            pe.wait_ge(S["cb_ev"], 1)

            for half in range(HALVES):
                base = half * HSTEPS
                pe.wait_ge(S["v0_r"], 2 * (half + 1))
                if half:
                    pe.wait_ge(S["y_ev"], half * HG)
                for n in range(STEPS):
                    k, o, r, w = n // OCT, n % OCT, (base + n) % 2, 2 ** (n // OCT)
                    pe.wait_ge(S["bdt_r"], base + n + 1)
                    if base + n >= 2:
                        pe.wait_ge(S["lvl_ev"], base + n - 1)
                    for j in range(8):
                        g = 8 * o + j
                        pe.matmul(pv_ps(r)[:, j, 0:w + NS], BDTa[:, r, j, :], PV[:, g, PW - w:PW + NS], start=True, stop=True)
                        mm = pe.matmul(w_ps(r)[:, j, 0:w], BDa[:, r, j, :], WP[:, g, L + 1 - w:L + 1], start=True, stop=True)
                    mm.then_inc(S["lvl_mm"], 1)
                pe.wait_ge(S["lvl_ev"], base + STEPS)
                pe.wait_ge(S["cm_r"], half + 1)
                for g in range(HG):
                    mm = pe.matmul(PS[:, 6, g * GC:(g + 1) * GC], PV[:, g, 0:L], CM[:, g, :], start=True, stop=True)
                mm.then_inc(S["k_mm"], 1)
                pe.wait_ge(S["k_sb"], half + 1)
                for b in range(2):
                    mm = pe.transpose(PS[:, 7, b * P:(b + 1) * P], ksb[:, b * P:(b + 1) * P], ident[:, :])
                mm.then_inc(S["kt_mm"], 1)
                pe.wait_ge(S["kt_r"], half + 1)

                def input_mats(q):
                    n = 8 * half + q
                    if q >= 2:
                        pe.wait_ge(S["ut_ev"], n - 1)
                    for i in range(4):
                        mm = pe.transpose(PS[:, 6 + q % 2, i * P:(i + 1) * P], PV[:, 4 * q + i, 0:L], ident[:, :])
                    mm.then_inc(S["ut_mm"], 1)

                if half == 0:
                    pe.wait_ge(S["xy_r"], NC)
                input_mats(0)
                for q in range(8):
                    n = 8 * half + q
                    if q < 7:
                        input_mats(q + 1)
                    pe.wait_ge(S["ut_ev"], n + 1)
                    if q >= 4:
                        pe.wait_ge(S["u_ev"], n - 3)
                    for i in range(4):
                        for e in range(4):
                            d = (half * HG + 4 * q + i) * GC + 2 * e
                            mm = pe.matmul(PS[32 * e:32 * e + 32, q % 4, i * P:(i + 1) * P],
                                           Uring[:, q % 2, i * P + 32 * e:i * P + 32 * e + 32], XY[:, d:d + 2, :],
                                           start=True, stop=True)
                    mm.then_inc(S["u_mm"], 1)
                pe.wait_ge(S["u_ev"], 8 * (half + 1))
                for i in range(SSTEPS):
                    k, o, n = i // OCT, i % OCT, base + STEPS + i
                    r = n % 2
                    pe.wait_ge(S["bdt_r"], n + 1)
                    if i >= 2:
                        pe.wait_ge(S["scan_h"], half * SSTEPS + i - 1)
                    for j in range(8):
                        g = 8 * o + j
                        mm = pe.matmul(pv_ps(r)[:, j, 0:NS + NC], BDTa[:, r, j, :], PV[:, g, H0:PW + NS], start=True, stop=True)
                        if k == 0:
                            mm = pe.matmul(w_ps(r)[:, j, 0:1], BDa[:, r, j, :], WP[:, g, L:L + 1], start=True, stop=True)
                    mm.then_inc(S["lvl_mm"], 1)
                pe.wait_ge(S["scan_h"], (half + 1) * SSTEPS)
                if half == HALVES - 1:
                    pe.wait_ge(S["ld_wo"], 16)
                    for q in range(QB):
                        if q >= 2:
                            pe.wait_ge(S["wo_ev"], q - 1)
                        for o in range(QB):
                            mm = pe.transpose(PS[:, 6 + q % 2, o * P:(o + 1) * P], WoN[:, o, q * P:(q + 1) * P], ident[:, :])
                        mm.then_inc(S["wo_tr"], 1)
                for g in range(HG):
                    n = half * HG + g
                    if g >= 4:
                        pe.wait_ge(S["y_ev"], n - 3)
                    pe.wait_ge(S["bdh_r"], n + 1)
                    if g == 0:
                        pe.wait_ge(S["bz_r"], half + 1)
                    pe.matmul(PS[:, g % 4, :], WP[:, g, 0:L], BDH[:, g % 2, :, :], start=True, stop=False,
                              skip_group_check=True).then_inc(S["o_mm"], 1)
                    pe.wait_ge(t_ld[n % 3], 16 * (n // 3 + 1))
                    for h in range(GC):
                        mm = pe.matmul(PS[:, g % 4, h * NC:(h + 1) * NC], Tring[:, n % 3, h, :], XY[:, n * GC + h, :],
                                       start=False, stop=(h == GC - 1), skip_group_check=True)
                    mm.then_inc(S["t_mm"], 1)

            pe.wait_ge(S["wo_ev"], QB)
            pe.wait_ge(S["y_ev"], NG)
            pe.wait_ge(S["ld_w"], 16 * 15)
            pe.wait_ge(S["prep_p"], 2)
            for r in range(2):
                for q in range(QB):
                    mm = pe.matmul(PS[64 * r:64 * r + 64, 5, 0:1], WinS[:, q, :], cbsb[:, 4 + q:5 + q], start=(q == 0), stop=(q == QB - 1))
                    if q == QB - 1 and r == 1:
                        mm.then_inc(S["prep_mm"], 1)

            def t_y(s, q):
                if q == 0:
                    pe.wait_ge(S["yh_r"], TPS * (s + 1))
                if q >= 2:
                    pe.wait_ge(S["gelu_r"], QB * s + q - 1)
                elif s >= 2:
                    pe.wait_ge(S["xT_r"], QB * (s - 2) + q + 3)
                for t in range(TPS):
                    mm = pe.transpose(PS[:, q % 2, t * P:(t + 1) * P], hatY[:, t, q * P:(q + 1) * P], ident[:, :])
                mm.then_inc(S["ty_mm"], 1)

            def out1(s, t):
                n = TPS * s + t
                if t == 0:
                    pe.wait_ge(S["gelu_r"], QB * (s + 1))
                if n >= 2:
                    pe.wait_ge(S["x2_r"], n - 1)
                for q in range(QB):
                    pe.matmul(PS[:, 2 + t % 2, :], zT[:, s % 2, q, t * P:(t + 1) * P], WoT[:, q, :], start=(q == 0), stop=False)
                pe.matmul(PS[:, 2 + t % 2, :], ones_bf[0:3, :], bias1[0:3, :], start=False, stop=True).then_inc(S["o1_mm"], 1)

            def out2(s, t):
                n = TPS * s + t
                if t == 0:
                    pe.wait_ge(S["ffn_r"], INNER * (s + 1))
                if n >= 2:
                    pe.wait_ge(S["x3_r"], n - 1)
                pe.matmul(PS[:, 6 + t % 2, :], gS[:, (t // 2) * P:(t // 2 + 1) * P], WoutS[:, t % 2, :], start=True, stop=False)
                pe.matmul(PS[:, 6 + t % 2, :], ones_bf[0:3, :], bias2[0:3, :], start=False, stop=True).then_inc(S["o2_mm"], 1)

            def t_x(s, q):
                if q == 0:
                    pe.wait_ge(S["xh2_r"], TPS * (s + 1))
                if q >= 2:
                    pe.wait_ge(S["xT_r"], QB * s + q - 1)
                else:
                    nxt = min(s + 1, NT - 1)
                    pe.wait_ge(S["gelu_r"], QB * nxt + q + 3)
                    if s == NT - 1:
                        pe.wait_ge(S["xT_r"], QB * (s - 1) + q + 3)
                for t in range(TPS):
                    mm = pe.transpose(PS[:, q % 2, t * P:(t + 1) * P], hatX[:, t, q * P:(q + 1) * P], ident[:, :])
                mm.then_inc(S["tx_mm"], 1)

            def s_prod(s, q):
                pe.wait_ge(S["xT_r"], QB * s + q + 1)
                if q == 0 and s >= 1:
                    pe.wait_ge(S["s_ev"], s)
                for t in range(TPS):
                    mm = pe.matmul(PS[:, 4, t * M:(t + 1) * M], x2T[:, q % 2, t * P:(t + 1) * P], WinS[:, q, :],
                                   start=(q == 0 and t == 0), stop=(q == QB - 1), skip_group_check=True)
                mm.then_inc(S["s_mm"], 1)

            def t_s(s):
                pe.wait_ge(S["s_ev"], s + 1)
                if s >= 1:
                    pe.wait_ge(S["relu_r"], INNER * s)
                for i in range(2):
                    mm = pe.transpose(PS[:, 5, i * P:(i + 1) * P], sS[:, i * P:(i + 1) * P], ident[:, :])
                mm.then_inc(S["st_mm"], 1)

            pe.wait_ge(S["prep_r"], 2)
            for q in range(QB):
                t_y(0, q)
            for s in range(NT):
                more = s + 1 < NT
                out1(s, 0)
                out1(s, 1)
                if more:
                    t_y(s + 1, 0)
                    t_y(s + 1, 1)
                out1(s, 2)
                if more:
                    t_y(s + 1, 2)
                    t_y(s + 1, 3)
                out1(s, 3)
                if s >= 1:
                    for t in range(TPS):
                        out2(s - 1, t)
                t_x(s, 0)
                t_x(s, 1)
                s_prod(s, 0)
                t_x(s, 2)
                s_prod(s, 1)
                t_x(s, 3)
                s_prod(s, 2)
                s_prod(s, 3)
                t_s(s)
            for t in range(TPS):
                out2(NT - 1, t)


def ones1(ident):
    return ident[0:1, 0:1]


def scan_add(dve, S, PV, pv_ps, half, base, i, ALU):
    k, o, n = i // OCT, i % OCT, base + STEPS + i
    w = 2 ** k
    dve.wait_ge(S["lvl_ev"], n + 1)
    st = PV[:, 8 * o:8 * o + 8, H0 + w:H0 + NC]
    dve.tensor_tensor(st, st, pv_ps(n % 2)[:, :, 0:NC - w], ALU.add).then_inc(S["scan_h"], 1)


_INS = ['L0_attn_x', 'L0_attn_A', 'L0_attn_Bm', 'L0_attn_Cm', 'L0_attn_Dm', 'L0_attn_ln_w', 'L0_attn_ln_b',
        'L0_attn_W_out', 'L0_attn_b_out', 'L0_ffn_Win', 'L0_ffn_bin_', 'L0_ffn_W1', 'L0_ffn_b1', 'L0_ffn_W2',
        'L0_ffn_b2', 'L0_ffn_Wout', 'L0_ffn_bout', 'L0_c', 'L0_wmod']


def kernel(**inputs):
    import numpy as _np
    import concourse.bacc as _bacc
    from concourse import mybir as _mybir
    from concourse.bass_utils import run_bass_kernel_spmd as _run

    nc = _bacc.Bacc("TRN2", target_bir_lowering=False, num_devices=1)
    arrays, args = {}, []
    for name in _INS:
        a = _np.ascontiguousarray(inputs[name])
        arrays[f"in_{name}"] = a
        args.append(nc.dram_tensor(f"in_{name}", a.shape, _mybir.dt.from_np(a.dtype), kind="ExternalInput").ap())
    res = nc.dram_tensor("out_0", (1, T, D), _mybir.dt.float32, kind="ExternalOutput").ap()
    adaln_ssm_kernel(nc, *args, res)
    r = _run(nc, [arrays], core_ids=[0])
    return r.results[0]["out_0"]
```

```python
import numpy as np
import concourse.bass as bass
from concourse import mybir
from contextlib import ExitStack


P = 128
D = 512
T = 8192
NS = 16
L = P
NC = T // L
GC = P // NS
NG = D // GC
HALVES = 2
HG = NG // HALVES
HD = D // HALVES
OCT = HG // 8
LEVELS = 7
PW = L
H0 = L - NC
SCANS = 6
STEPS = LEVELS * OCT
SSTEPS = SCANS * OCT
HSTEPS = STEPS + SSTEPS
QB = D // P
M = 64
INNER = 16
EPS = 1e-5
TPS = 4
NT = NC // TPS
TPU = 2
NU = NC // TPU
UW = TPU * P
XS = 5
RELU_RING = 4
XR = 10
LNB = 4
LNA = 7
MODE = 5
BDR = 4
QD = range(0, P, 2 * NS)


def adaln_ssm_kernel(nc, x_in, A_in, Bm_in, Cm_in, Dm_in, lnw_in, lnb_in, Wo_in, bo_in,
                     Win_in, bin_in, W1_in, b1_in, W2_in, b2_in, Wout_in, bout_in, c_in, wmod_in, out):
    f32 = mybir.dt.float32
    bf16 = mybir.dt.bfloat16
    ALU = mybir.AluOpType
    ACT = mybir.ActivationFunctionType
    AX = mybir.AxisListType

    kscr = nc.dram_tensor("kernel_taps", [D, 2 * L], f32, kind="Internal").ap()
    x_t = x_in[0].rearrange("(c p) d -> p c d", p=P)
    out_t = out[0].rearrange("(c p) d -> p c d", p=P)

    ctx = ExitStack()
    with ctx:
        def sb(name, shape, dt=f32):
            return ctx.enter_context(nc.sbuf_tensor(name, shape, dt))

        def sem(name):
            return ctx.enter_context(nc.semaphore(name))

        XY = sb("XY", [P, D, NC])
        A0 = sb("arenaA", [P, 8736])
        PV = A0[:, 0:HG * 144].rearrange("p (g w) -> p g w", w=144)
        WP = A0[:, 4608:4608 + HG * 129].rearrange("p (g w) -> p g w", w=129)
        C0 = sb("arenaC", [P, 8192])
        BDs = C0[:, 0:1024].rearrange("p (r g m) -> p r g m", r=BDR, g=8)
        BDTs = C0[:, 1024:2048].rearrange("p (r g m) -> p r g m", r=BDR, g=8)
        UR = C0[:, 2048:3072]
        ROWS = sb("ROWS", [P, 4, D])
        ident = sb("ident", [P, P])
        bcs = sb("bcs", [P, 256])
        mask8 = sb("mask8", [P, GC])
        par = sb("par", [P, 2])
        ST = sb("ST", [P, 3, NC])
        ccol = sb("ccol", [P, QB])
        DmT = sb("DmT", [P, QB])
        cbsb = sb("cbsb", [P, 2 * QB])
        lnwb = sb("lnwb", [P, 2 * QB])
        bs6 = sb("bs6", [P, 4, 6])
        half_neg = sb("half_neg", [P, 8])

        CA1, SA, GA, GB = (ROWS[:, i, :] for i in range(4))
        mean_x, rstd_x, nmr_x = (ST[:, i, :] for i in range(3))
        wm_first = XY[:, 0:2 * 4 * 8, :].rearrange("p (j k r) c -> p j k (r c)", j=2, k=4)
        wm_later = C0[:, 6144:8192].rearrange("p (k n) -> p k n", k=4)
        crep = GB.rearrange("p (k m) -> p k m", k=4)
        sgn = C0[:, 6144:6144 + D]
        bcn = bcs[:, 0:128]
        BCT = bcs[:, 128:256]
        CM = UR[:, 0:256].rearrange("p (g c) -> p g c", c=GC)
        ksb = UR[:, 256:512]
        ktz = UR[:, 512:1024].rearrange("p (b w) -> p b w", b=2)
        Uring = UR.rearrange("p (r w) -> p r w", r=2)
        BDH = UR.rearrange("p (r h c) -> p r h c", r=2, h=GC)
        Tring = C0[:, 3072:6144].rearrange("p (r h i) -> p r h i", r=3, h=GC)
        xst = C0[:, 3072:3072 + XR * D].rearrange("p (r d) -> p r d", r=XR)
        zT = A0[:, 0:2048].rearrange("p (r q t) -> p r q t", r=2, q=QB)
        hatX = A0[:, 2048:4096].rearrange("p (r t d) -> p r t d", r=2, t=TPU)
        x2T = A0[:, 4096:6144].rearrange("p (r q t) -> p r q t", r=2, q=QB)
        gS = A0[:, 6144:6400].rearrange("p (r t) -> p r t", r=2)
        hatY = C0[:, 0:2048].rearrange("p (r t d) -> p r t d", r=2, t=TPU)
        xr = [C0[:, 2048 + 1024 * i:3072 + 1024 * i].rearrange("p (t d) -> p t d", t=TPU) for i in range(4)]
        xr.append(A0[:, 6400:7424].rearrange("p (t d) -> p t d", t=TPU))
        WoN = C0[:, 0:2048].rearrange("p (o d) -> p o d", o=QB)
        WoT = C0[:, 6144:8192].rearrange("p (q d) -> p q d", q=QB)
        Grow = CA1
        tmp = SA
        rr = GA.rearrange("p (r t) -> p r t", r=RELU_RING)
        b1row, b2row = C0[:, 0:512], C0[:, 512:1024]
        part = C0[:, 1024:1280].bitcast(bf16)
        WoutN = C0[:, 1280:1792]
        WoutS = GB
        WinS = sb("WinS", [P, QB, M])
        bias1 = sb("bias1", [P, D], bf16)
        bias2 = bcs[:, 0:256].bitcast(bf16)
        ones_bf = sb("ones_bf", [P, P], bf16)
        ffc = sb("ffc", [P, 3 * INNER + 4])
        W1c, b1c, W2c = (ffc[:, i * INNER:(i + 1) * INNER] for i in range(3))
        b2c, binc = ffc[:, 48:49], ffc[:, 49:50]
        bx6 = sb("bx6", [P, TPU, 6])
        mvy = sb("mvy", [P, TPS, 2])
        mvx = sb("mvx", [P, 2, TPU, 2])
        sy = sb("sy", [P, 2, 2, TPS])
        s2 = sb("s2", [P, 2, 2, TPU])

        PS = ctx.enter_context(nc.psum_tensor("PS", [P, 8, 512], f32))

        def pv_ps(r):
            return PS[:, 2 * r:2 * r + 2, :].rearrange("p b (s w) -> p (b s) w", w=128)

        def w_ps(r):
            return PS[:, 4 + r, :].rearrange("p (g w) -> p g w", w=64)

        S = {}
        for name in ("consts", "ident_r", "ld_c", "ld_bc", "ld_A", "ld_small", "silu_r", "crep_r", "mod_mm", "mod_ev", 
                     "bct_mm", "bct_ev", "par_r", "v0_r", "w0_r",
                     "bn_r", "rst_r", "xh_r", "xm_r", "xy_r", "dchain", "pchain",
                     "bd_r", "bdt_r", "lvl_mm", "lvl_ev", "scan_h", "cm_r", "kz_r", "k_mm", "k_sb", "kt_mm", "kt_r", "k_saved",
                     "ut_mm", "ut_ev", "u_mm", "u_ev", "bdh_r", "o_mm", "t_mm", "y_ev", "bz_r",
                     "ld_wo", "wo_tr", "wo_ev", "ld_w", "prep_r", "prep_mm",
                     "ty_mm", "gelu_r", "o1_mm", "x2_r", "yst", "yr_r", "yh_r", "x2st", "x2rs", "xh2_r", "tx_mm", "xT_r",
                     "s_mm", "relu_r", "ffn_r", "o2_mm", "x3_r", "xres_r"):
            S[name] = sem(name)
        ld_wm = [sem(f"ld_wm{j}") for j in range(6)]
        x_ld = [sem(f"x_ld{r}") for r in range(XR)]
        t_ld = [sem(f"t_ld{r}") for r in range(3)]
        xc_ld = [sem(f"xc_ld{r}") for r in range(XS)]
        x_st = [sem(f"x_st{r}") for r in range(XS)]

        MOD_ORDER = [1, 0, 4, 3, 2, 5]

        def tiles_of(n):
            return range(NC * n // STEPS, NC * (n + 1) // STEPS)

        block = ctx.enter_context(nc.Block())

        @block.sync
        def _(sp):
            with nc.allow_non_contiguous_dma(reason="columns of a few hundred elements"):
                sp.dma_start(ccol[:, :], c_in[0].rearrange("(k p) -> p k", p=P)).then_inc(S["ld_c"], 16)
                sp.dma_start(bcn[0:64, :], Bm_in.rearrange("(g c) n -> g (c n)", c=GC)).then_inc(S["ld_bc"], 16)
                sp.dma_start(bcn[64:128, :], Cm_in.rearrange("(g c) n -> g (c n)", c=GC)).then_inc(S["ld_bc"], 16)
                wv = wmod_in.rearrange("(k p) n -> p k n", p=P)
                for i in range(2):
                    j = MOD_ORDER[i]
                    sp.dma_start(wm_first[:, i, :, :], wv[:, :, j * D:(j + 1) * D]).then_inc(ld_wm[j], 16)
            Av = A_in.rearrange("(g c) n m -> (c n) g m", c=GC)

            def load_A(half):
                sp.dma_start(PV[:, :, PW:PW + NS], Av[:, half * HG:(half + 1) * HG, :]).then_inc(S["ld_A"], 16)

            load_A(0)
            with nc.allow_non_contiguous_dma(reason="columns of a few hundred elements"):
                sp.dma_start(DmT[:, :], Dm_in.rearrange("(k p) -> p k", p=P)).then_inc(S["ld_small"], 16)
                sp.dma_start(lnwb[:, 0:QB], lnw_in.rearrange("(k p) -> p k", p=P)).then_inc(S["ld_small"], 16)
                sp.dma_start(lnwb[:, QB:], lnb_in.rearrange("(k p) -> p k", p=P)).then_inc(S["ld_small"], 16)

            def load_x(c):
                if c >= XR:
                    sp.wait_ge(S["xh_r"], c - XR + 1)
                sp.dma_start(xst[:, c % XR, :], x_t[:, c, :]).then_inc(x_ld[c % XR], 16)

            for c in range(NC):
                load_x(c)
            def load_last_weights():
                sp.wait_ge(S["wo_tr"], QB)
                with nc.allow_non_contiguous_dma(reason="columns of a few hundred elements"):
                    sp.dma_start(WinS[:, :, :], Win_in.rearrange("(q p) m -> p q m", p=P)).then_inc(S["ld_w"], 16)
                    sp.dma_start(b1row, bo_in.partition_broadcast(P)).then_inc(S["ld_w"], 16)
                    sp.dma_start(b2row, bout_in.partition_broadcast(P)).then_inc(S["ld_w"], 16)
                    for r in range(2):
                        sp.dma_start(WoutN[64 * r:64 * r + 64, :], Wout_in).then_inc(S["ld_w"], 16)
                        for dst, src in ((W1c, W1_in), (b1c, b1_in), (W2c, W2_in)):
                            sp.dma_start(dst[64 * r:64 * r + 64, :], src).then_inc(S["ld_w"], 16)
                        sp.dma_start(b2c[64 * r:64 * r + 64, :], b2_in.rearrange("(m a) -> m a", a=1)).then_inc(S["ld_w"], 16)
                        sp.dma_start(binc[64 * r:64 * r + 64, :], bin_in.rearrange("(m a) -> m a", a=1)).then_inc(S["ld_w"], 16)

            for half in range(HALVES):
                if half:
                    sp.wait_ge(S["o_mm"], half * HG)
                    sp.wait_ge(S["bdh_r"], half * HG)
                    load_A(half)
                sp.wait_ge(S["kt_r"], half + 1)
                sp.dma_start(kscr[half * HD:(half + 1) * HD, :].rearrange("(b p) w -> p b w", p=P), ktz).then_inc(S["k_saved"], 16)
                sp.wait_ge(S["k_saved"], 16 * (half + 1))
                if half == 0:
                    sp.wait_ge(S["xy_r"], NC)
                    for i in range(2, 6):
                        j = MOD_ORDER[i]
                        if i > 2:
                            sp.wait_ge(S["mod_ev"], i)
                        sp.dma_start(wm_later, wv[:, :, j * D:(j + 1) * D]).then_inc(ld_wm[j], 16)
                for g in range(HG):
                    n = half * HG + g
                    if n >= 3:
                        sp.wait_ge(S["t_mm"], n - 2)
                    row = (half * HG + g) * GC
                    src = bass.AP(kscr.tensor, row * 2 * L, [[1, P], [2 * L, GC], [1, L]])
                    sp.dma_start(Tring[:, n % 3, :, :], src).then_inc(t_ld[n % 3], 16)
                    if half == HALVES - 1 and g == 0:
                        sp.wait_ge(S["lvl_mm"], HALVES * HSTEPS)
                        sp.dma_start(WoN, Wo_in.rearrange("(o p) d -> p o d", p=P)).then_inc(S["ld_wo"], 16)
                    if half == HALVES - 1 and g == 2:
                        load_last_weights()
            sp.wait_ge(S["t_mm"], NG)
            sp.wait_ge(S["bdh_r"], NG)

            def load_unit(u):
                sp.dma_start(xr[u % XS], x_t[:, u * TPU:(u + 1) * TPU, :]).then_inc(xc_ld[u % XS], 16)

            for u in range(XS):
                load_unit(u)
            for u in range(NU):
                b = u % XS
                sp.wait_ge(S["x3_r"], TPU * (u + 1))
                sp.dma_start(out_t[:, u * TPU:(u + 1) * TPU, :], xr[b]).then_inc(x_st[b], 16)
                if u + XS < NU:
                    sp.wait_ge(x_st[b], 16 * (u // XS + 1))
                    load_unit(u + XS)
            for b in range(XS):
                sp.wait_ge(x_st[b], 16 * ((NU - 1 - b) // XS + 1))

        @block.gpsimd
        def _(gp):
            nch = [0]

            def chain(ins):
                nch[0] += 1
                ins.then_inc(S["pchain"], 1)
                gp.wait_ge(S["pchain"], nch[0])

            chain(gp.memset(ident[:, :], 0.0))
            gp.affine_select(out=ident[:, :], in_=ident[:, :], compare_op=ALU.not_equal, fill=1.0, base=0,
                             pattern=[[-1, P]], channel_multiplier=1).then_inc(S["ident_r"], 1)
            gp.memset(half_neg[:, :], -0.5).then_inc(S["consts"], 1)
            gp.memset(ones_bf[:, :], 1.0).then_inc(S["consts"], 1)
            chain(gp.memset(mask8[:, :], 1.0))
            chain(gp.affine_select(out=mask8[:, :], in_=mask8[:, :], compare_op=ALU.is_ge, fill=0.0, base=0,
                                   pattern=[[-NS, GC]], channel_multiplier=1))
            gp.affine_select(out=mask8[:, :], in_=mask8[:, :], compare_op=ALU.is_ge, fill=0.0, base=NS - 1,
                             pattern=[[NS, GC]], channel_multiplier=-1).then_inc(S["consts"], 1)
            gp.wait_ge(S["consts"], 3)

            def rstd_of(var, mean, rstd, nmr, w, done):
                chain(gp.tensor_scalar(rstd, var, EPS, 0.0, ALU.add, ALU.add))
                chain(gp.tensor_tensor(rstd, rstd, half_neg[:, 0:w], ALU.pow))
                chain(gp.tensor_tensor(nmr, mean, rstd, ALU.mult))
                gp.tensor_scalar(nmr, nmr, -1.0, 0.0, ALU.mult, ALU.add).then_inc(done, 1)

            def scale_x(c):
                gp.wait_ge(S["xh_r"], c + 1)
                if c == 0:
                    gp.wait_ge(S["mod_ev"], 1)
                gp.tensor_tensor(XY[:, :, c], XY[:, :, c], CA1, ALU.mult).then_inc(S["xm_r"], 1)

            for half in range(HALVES):
                base = half * HSTEPS
                for n in range(STEPS):
                    if half == 0:
                        for c in tiles_of(n):
                            c1 = 0 if c == 0 else c + 2
                            if c1 % LNB == 0 and c1 < NC:
                                gp.wait_ge(S["bn_r"], c1 + LNB)
                                cc = slice(c1, c1 + LNB)
                                rstd_of(rstd_x[:, cc], mean_x[:, cc], rstd_x[:, cc], nmr_x[:, cc], LNB, S["rst_r"])
                            if c >= 1:
                                scale_x(c - 1)
                    if n == 1:
                        if half == 0:
                            gp.wait_ge(S["bct_ev"], 1)
                        else:
                            gp.wait_ge(S["o_mm"], half * HG)
                        cb = BCT[:, 64 + half * HG:64 + (half + 1) * HG].unsqueeze(2).to_broadcast([P, HG, GC])
                        gp.tensor_tensor(CM, cb, mask8[:, :].unsqueeze(1).to_broadcast([P, HG, GC]), ALU.mult).then_inc(S["cm_r"], 1)
                        gp.memset(ktz, 0.0).then_inc(S["kz_r"], 1)
                if half == 0:
                    scale_x(NC - 1)
                gp.wait_ge(S["u_mm"], 8 * (half + 1))
                gp.memset(BDH[:, :, :, 0:1], 0.0).then_inc(S["bz_r"], 1)
                for g in range(HG):
                    n = half * HG + g
                    if g % 8 == 0:
                        gp.wait_ge(S["scan_h"], half * SSTEPS + SSTEPS - OCT + g // 8 + 1)
                    if g >= 2:
                        gp.wait_ge(S["o_mm"], n - 1)
                    gp.tensor_tensor(BDH[:, g % 2, :, 1:NC], PV[:, g, H0:H0 + NC - 1].unsqueeze(1).to_broadcast([P, GC, NC - 1]),
                                     mask8[:, :].unsqueeze(2).to_broadcast([P, GC, NC - 1]), ALU.mult).then_inc(S["bdh_r"], 1)

            def rstd_y(v):
                gp.wait_ge(S["yst"], v + 1)
                if v >= 2:
                    gp.wait_ge(S["yh_r"], TPS * (v - 1))
                rstd_of(mvy[:, :, 1], mvy[:, :, 0], sy[:, v % 2, 0, :], sy[:, v % 2, 1, :], TPS, S["yr_r"])

            def residual(u):
                gp.wait_ge(xc_ld[u % XS], 16 * (u // XS + 1))
                for t in range(TPU):
                    c = TPU * u + t
                    chain(gp.tensor_scalar(tmp, xr[u % XS][:, t, :], rstd_x[:, c:c + 1], nmr_x[:, c:c + 1], ALU.mult, ALU.add))
                    chain(gp.tensor_tensor(tmp, tmp, Grow, ALU.mult))
                    gp.tensor_tensor(xr[u % XS][:, t, :], xr[u % XS][:, t, :], tmp, ALU.add).then_inc(S["xres_r"], 1)
                    gp.wait_ge(S["xres_r"], c + 1)

            gp.wait_ge(S["prep_r"], 2)
            rstd_y(0)
            residual(0)
            rstd_y(1)
            residual(1)
            for u in range(NU):
                gp.wait_ge(S["x2st"], u + 1)
                if u >= 2:
                    gp.wait_ge(S["xh2_r"], TPU * (u - 1))
                r = u % 2
                rstd_of(mvx[:, r, :, 1], mvx[:, r, :, 0], s2[:, r, 0, :], s2[:, r, 1, :], TPU, S["x2rs"])
                if u % 2 and u // 2 + 2 < NT:
                    rstd_y(u // 2 + 2)
                if u + 2 < NU:
                    residual(u + 2)

        @block.scalar
        def _(act):
            act.wait_ge(S["ld_c"], 16)
            act.activation(ccol[:, :], ccol[:, :], ACT.Silu).then_inc(S["silu_r"], 1)
            act.wait_ge(S["bct_mm"], 1)
            act.activation(BCT, PS[:, 7, 0:128], ACT.Copy).then_inc(S["bct_ev"], 1)
            act.wait_ge(S["bct_ev"], 1)

            def normalise_x(c):
                act.wait_ge(S["rst_r"], c // LNB + 1)
                if c == 0:
                    act.wait_ge(S["mod_mm"], 2)
                act.activation(XY[:, :, c], xst[:, c % XR, :], ACT.Identity, scale=rstd_x[:, c:c + 1],
                               bias=nmr_x[:, c:c + 1]).then_inc(S["xh_r"], 1)

            for half in range(HALVES):
                base = half * HSTEPS
                if half:
                    act.wait_ge(S["o_mm"], half * HG)
                    act.wait_ge(S["bdh_r"], half * HG)
                act.activation(PV[:, :, PW - 1], BCT[:, half * HG:(half + 1) * HG], ACT.Copy).then_inc(S["v0_r"], 1)
                act.activation(WP[:, :, L], BCT[:, 64 + half * HG:64 + (half + 1) * HG], ACT.Copy).then_inc(S["v0_r"], 1)
                for c in tiles_of(0) if half == 0 else ():
                    normalise_x(c)
                for n in range(STEPS):
                    if half == 0 and n + 1 < STEPS:
                        for c in tiles_of(n + 1):
                            normalise_x(c)
                    k, o, r, w = n // OCT, n % OCT, (base + n) % 2, 2 ** (n // OCT)
                    act.wait_ge(S["lvl_mm"], base + n + 1)
                    act.activation(PV[:, 8 * o:8 * o + 8, PW:PW + NS], pv_ps(r)[:, :, w:w + NS], ACT.Copy)
                    act.activation(PV[:, 8 * o:8 * o + 8, PW - 2 * w:PW - w], pv_ps(r)[:, :, 0:w], ACT.Copy)
                    act.activation(WP[:, 8 * o:8 * o + 8, L + 1 - 2 * w:L + 1 - w], w_ps(r)[:, :, 0:w], ACT.Copy).then_inc(S["lvl_ev"], 1)
                for q in range(8):
                    n = 8 * half + q
                    act.wait_ge(S["ut_mm"], n + 1)
                    if q == 0:
                        act.wait_ge(S["k_saved"], 16 * (half + 1))
                    if q >= 2:
                        act.wait_ge(S["u_mm"], n - 1)
                    act.activation(Uring[:, q % 2, :], PS[:, 6 + q % 2, :], ACT.Copy).then_inc(S["ut_ev"], 1)
                for i in range(SSTEPS):
                    k, o, n = i // OCT, i % OCT, base + STEPS + i
                    r = n % 2
                    act.wait_ge(S["lvl_mm"], n + 1)
                    if k == 0:
                        act.activation(WP[:, 8 * o:8 * o + 8, 0], w_ps(r)[:, :, 0], ACT.Copy)
                    act.activation(PV[:, 8 * o:8 * o + 8, PW:PW + NS], pv_ps(r)[:, :, NC:NC + NS], ACT.Copy).then_inc(S["lvl_ev"], 1)
                for g in range(HG):
                    n = half * HG + g
                    act.wait_ge(S["t_mm"], n + 1)
                    d = n * GC
                    act.activation(XY[:, d:d + GC, :], PS[:, g % 4, :].rearrange("p (h c) -> p h c", h=GC),
                                   ACT.Copy).then_inc(S["y_ev"], 1)

            def yhat(u):
                v = u * TPU // TPS
                act.wait_ge(S["yr_r"], v + 1)
                if u >= 2:
                    act.wait_ge(S["ty_mm"], 2 * (u - 1))
                for t in range(TPU):
                    i = (u * TPU + t) % TPS
                    act.activation(hatY[:, u % 2, t, :], XY[:, :, u * TPU + t], ACT.Identity, scale=sy[:, v % 2, 0, i:i + 1],
                                   bias=sy[:, v % 2, 1, i:i + 1]).then_inc(S["yh_r"], 1)

            def gelu(u):
                if u >= 2:
                    act.wait_ge(S["o1_mm"], TPU * (u - 1))
                for q in range(QB):
                    act.wait_ge(S["ty_mm"], 2 * u + q // 2 + 1)
                    act.activation(zT[:, u % 2, q, :].rearrange("p (t i) -> p t i", i=P),
                                   PS[:, q // 2, (q % 2) * UW:(q % 2 + 1) * UW].rearrange("p (t i) -> p t i", i=P)[:, :, ::-1],
                                   ACT.Gelu, scale=lnwb[:, q:q + 1], bias=lnwb[:, QB + q:QB + q + 1]).then_inc(S["gelu_r"], 1)

            def xhat2(u):
                act.wait_ge(S["x2rs"], u + 1)
                if u >= 2:
                    act.wait_ge(S["tx_mm"], 2 * (u - 1))
                for t in range(TPU):
                    act.activation(hatX[:, u % 2, t, :], xr[u % XS][:, t, :], ACT.Identity, scale=s2[:, u % 2, 0, t:t + 1],
                                   bias=s2[:, u % 2, 1, t:t + 1]).then_inc(S["xh2_r"], 1)

            def x2_columns(u):
                if u >= 2:
                    act.wait_ge(S["s_mm"], u - 1)
                for b in range(2):
                    act.wait_ge(S["tx_mm"], 2 * u + b + 1)
                    act.activation(x2T[:, u % 2, 2 * b:2 * b + 2, :].rearrange("p q t -> p (q t)"), PS[:, 4, :],
                                   ACT.Copy).then_inc(S["xT_r"], 1)

            def relus(u):
                act.wait_ge(S["s_mm"], u + 1)
                for h in range(INNER):
                    n = INNER * u + h
                    if n >= RELU_RING:
                        act.wait_ge(S["ffn_r"], n - RELU_RING + 1)
                    act.activation(rr[:, h % RELU_RING, :], PS[:, 5, 0:P], ACT.Relu, scale=W1c[:, h:h + 1],
                                   bias=b1c[:, h:h + 1]).then_inc(S["relu_r"], 1)

            act.wait_ge(S["ld_small"], 48)
            act.wait_ge(S["prep_r"], 2)
            yhat(0)
            gelu(0)
            yhat(1)
            for u in range(NU + 1):
                if u >= 1:
                    xhat2(u - 1)
                if u + 1 < NU:
                    gelu(u + 1)
                if u >= 1:
                    x2_columns(u - 1)
                if u + 2 < NU:
                    yhat(u + 2)
                if u >= 1:
                    relus(u - 1)

        @block.vector
        def _(dve):
            nch = [0]

            def chain(ins):
                nch[0] += 1
                ins.then_inc(S["dchain"], 1)
                dve.wait_ge(S["dchain"], nch[0])

            dve.wait_ge(S["silu_r"], 1)
            dve.tensor_copy(crep, ccol[:, :].unsqueeze(2).to_broadcast([P, QB, P])).then_inc(S["crep_r"], 1)
            dve.wait_ge(S["consts"], 3)
            for e in range(2):
                dve.reduce_sum(par[:, e:e + 1], mask8[:, e::2], AX.X).then_inc(S["par_r"], 1)
            dve.wait_ge(S["par_r"], 2)

            def mod_rows(which):
                for i in which:
                    j = MOD_ORDER[i]
                    dve.wait_ge(S["mod_mm"], i + 1)
                    src = PS[:, 6 + i % 2, :]
                    if j == 1:
                        dve.tensor_scalar(CA1, src, 1.0, None, ALU.add).then_inc(S["mod_ev"], 1)
                    elif j == 0:
                        dve.tensor_copy(SA, src).then_inc(S["mod_ev"], 1)
                    elif j in (2, 5):
                        row = GA if j == 2 else GB
                        dve.tensor_scalar(sgn, src, 0.0, 2.0, ALU.is_ge, ALU.mult)
                        chain(dve.tensor_scalar(row, src, -1.0, 0.25, ALU.mult, ALU.max))
                        chain(dve.tensor_tensor(row, row, src, ALU.max))
                        ins = dve.scalar_tensor_tensor(out=row, in0=sgn, scalar=-1.0, in1=row, op0=ALU.add, op1=ALU.mult)
                        ins.then_inc(S["mod_ev"], 1)
                        dve.wait_ge(S["mod_ev"], i + 1)
                    elif j == 4:
                        dve.tensor_scalar(cbsb[:, 0:QB], src[:, 0:QB], 1.0, None, ALU.add).then_inc(S["mod_ev"], 1)
                    else:
                        dve.tensor_copy(cbsb[:, QB:], src[:, 0:QB]).then_inc(S["mod_ev"], 1)

            def stats_x(c):
                dve.wait_ge(x_ld[c % XR], 16 * (c // XR + 1))
                if c >= 4:
                    dve.wait_ge(S["bn_r"], c - 3)
                chain(dve.bn_stats(bs6[:, c % 4, :], xst[:, c % XR, :]))
                dve.bn_aggr(ST[:, 0:2, c], bs6[:, c % 4, :]).then_inc(S["bn_r"], 1)

            def shift_x(c):
                dve.wait_ge(S["xm_r"], c + 1)
                dve.tensor_tensor(XY[:, :, c], XY[:, :, c], SA, ALU.add).then_inc(S["xy_r"], 1)

            def power_mats(half, k, o, n):
                if k == 0:
                    if o == 0:
                        dve.wait_ge(S["ld_A"], 16 * (half + 1))
                else:
                    dve.wait_ge(S["lvl_ev"], n - OCT + 1)
                if n >= BDR:
                    dve.wait_ge(S["lvl_mm"], n - BDR + 1)
                src = PV[:, 8 * o:8 * o + 8, PW:PW + NS].unsqueeze(2).to_broadcast([P, 8, 2, NS])
                msk = par[:, :].unsqueeze(1).unsqueeze(3).to_broadcast([P, 8, 2, NS])
                dve.tensor_tensor(BDs[:, n % BDR, :, :].rearrange("p g (a m) -> p g a m", m=NS), src, msk,
                                  ALU.mult).then_inc(S["bd_r"], 1)
                dve.wait_ge(S["bd_r"], n + 1)
                dve.transpose(BDTs[:, n % BDR, :, :], BDs[:, n % BDR, :, :]).then_inc(S["bdt_r"], 1)

            for half in range(HALVES):
                base = half * HSTEPS
                for n in range(STEPS):
                    if n == 0 and half == 0:
                        for c in range(LNA):
                            stats_x(c)
                        mod_rows(range(2))
                    power_mats(half, n // OCT, n % OCT, base + n)
                    if half == 0:
                        for c in tiles_of(n):
                            if c + LNA < NC:
                                stats_x(c + LNA)
                            if c >= 2:
                                shift_x(c - 2)
                if half == 0:
                    for c in (NC - 2, NC - 1):
                        shift_x(c)
                dve.wait_ge(S["k_mm"], half + 1)
                dve.tensor_copy(ksb, PS[:, 6, 0:HD]).then_inc(S["k_sb"], 1)
                dve.wait_ge(S["kt_mm"], half + 1)
                dve.wait_ge(S["kz_r"], half + 1)
                if half == 0:
                    dve.wait_ge(S["ld_small"], 48)
                chain(dve.tensor_copy(ktz[:, :, 0:L], PS[:, 7, 0:HD].rearrange("p (b w) -> p b w", b=2)))
                dve.tensor_tensor(ktz[:, :, L - 1], ktz[:, :, L - 1], DmT[:, 2 * half:2 * half + 2], ALU.add).then_inc(S["kt_r"], 1)
                for q in range(8):
                    n = 8 * half + q
                    dve.wait_ge(S["u_mm"], n + 1)
                    ps = PS[:, q % 4, :].rearrange("p (g a c) -> p g a c", g=4, a=2)
                    st = PV[:, 4 * q:4 * q + 4, H0:H0 + NC]
                    chain(dve.tensor_scalar(st, ps[:, :, 0, :], par[:, 0:1], None, ALU.mult))
                    dve.scalar_tensor_tensor(out=st, in0=ps[:, :, 1, :], scalar=par[:, 1:2], in1=st, op0=ALU.mult,
                                             op1=ALU.add).then_inc(S["u_ev"], 1)
                dve.wait_ge(S["u_ev"], 8 * (half + 1))
                for i in range(SSTEPS):
                    k, o, n = i // OCT, i % OCT, base + STEPS + i
                    power_mats(half, LEVELS + k, o, n)
                    if i >= 1:
                        scan_add(dve, S, PV, pv_ps, half, base, i - 1, ALU)
                    if half == 0 and i % MODE == MODE - 1 and i // MODE < 4:
                        mod_rows((2 + i // MODE,))
                scan_add(dve, S, PV, pv_ps, half, base, SSTEPS - 1, ALU)

            for q in range(QB):
                dve.wait_ge(S["wo_tr"], q + 1)
                dve.tensor_tensor(WoT[:, q, :], PS[:, 6 + q % 2, :], GA, ALU.mult).then_inc(S["wo_ev"], 1)

            dve.wait_ge(S["ld_w"], 16 * 15)
            dve.wait_ge(S["prep_mm"], 1)
            dve.tensor_tensor(binc, binc, PS[:, 5, 0:1], ALU.add).then_inc(S["dchain"], 1)
            for q in range(QB):
                dve.tensor_scalar(WinS[:, q, :], WinS[:, q, :], cbsb[:, q:q + 1], None, ALU.mult).then_inc(S["dchain"], 1)
            dve.tensor_tensor(b1row, b1row, SA, ALU.add).then_inc(S["dchain"], 1)
            dve.tensor_tensor(b2row, b2row, GB, ALU.mult).then_inc(S["dchain"], 1)
            dve.tensor_tensor(Grow, CA1, GA, ALU.mult).then_inc(S["dchain"], 1)
            nch[0] += 1 + QB + 3
            dve.wait_ge(S["dchain"], nch[0])
            chain(dve.scalar_tensor_tensor(out=b1c, in0=W1c, scalar=binc, in1=b1c, op0=ALU.mult, op1=ALU.add))
            chain(dve.tensor_tensor(WoutS, WoutN, GB, ALU.mult))
            chain(dve.tensor_tensor(b1row, b1row, GA, ALU.mult))
            up, acc = PS[:, 7, :], tmp
            for rest, dst in ((b1row, bias1[:, :]), (b2row, bias2)):
                for i in range(3):
                    chain(dve.tensor_copy(part, rest))
                    chain(dve.tensor_copy(up, part))
                    if i == 0:
                        chain(dve.tensor_scalar(acc, up, ident[:, i:i + 1], None, ALU.mult))
                    else:
                        chain(dve.scalar_tensor_tensor(out=acc, in0=up, scalar=ident[:, i:i + 1], in1=acc, op0=ALU.mult, op1=ALU.add))
                    chain(dve.tensor_tensor(rest, rest, up, ALU.subtract))
                chain(dve.tensor_copy(dst, acc))
            dve.memset(bs6[:, 0, 0:1], 0.0).then_inc(S["prep_r"], 2)
            dve.wait_ge(S["prep_r"], 2)

            def y_stats(v, ts):
                if v >= 1 and ts[0] == 0:
                    dve.wait_ge(S["yst"], v)
                for t in ts:
                    dve.bn_stats(bs6[:, t, :], XY[:, :, v * TPS + t]).then_inc(S["dchain"], 1)
                nch[0] += len(ts)
                if ts[-1] == TPS - 1:
                    dve.wait_ge(S["dchain"], nch[0])
                    if v >= 1:
                        dve.wait_ge(S["yr_r"], v)
                    for t in range(TPS):
                        ins = dve.bn_aggr(mvy[:, t, :], bs6[:, t, :])
                    ins.then_inc(S["yst"], 1)

            def first_residual(u, t):
                n = TPU * u + t
                x2 = xr[u % XS][:, t, :]
                dve.wait_ge(S["o1_mm"], n + 1)
                dve.wait_ge(S["xres_r"], n + 1)
                dve.tensor_tensor(x2, x2, PS[:, 2 + t, :], ALU.add).then_inc(S["x2_r"], 1)
                dve.wait_ge(S["x2_r"], n + 1)
                if u >= 1:
                    dve.wait_ge(S["x2st"], u)
                ins = dve.bn_stats(bx6[:, t, :], x2)
                if t < TPU - 1:
                    nch[0] += 1
                    ins.then_inc(S["dchain"], 1)
                    return
                chain(ins)
                if u >= 2:
                    dve.wait_ge(S["x2rs"], u - 1)
                for i in range(TPU):
                    ins = dve.bn_aggr(mvx[:, u % 2, i, :], bx6[:, i, :])
                ins.then_inc(S["x2st"], 1)

            def ffn(u):
                g = gS[:, u % 2, :]
                for h in range(INNER):
                    n = INNER * u + h
                    dve.wait_ge(S["relu_r"], n + 1)
                    if h == 0:
                        if u >= 2:
                            dve.wait_ge(S["o2_mm"], TPU * (u - 1))
                        ins = dve.tensor_scalar(g, rr[:, 0, :], W2c[:, 0:1], b2c, ALU.mult, ALU.add)
                    else:
                        dve.wait_ge(S["ffn_r"], n)
                        ins = dve.scalar_tensor_tensor(out=g, in0=rr[:, h % RELU_RING, :], scalar=W2c[:, h:h + 1],
                                                       in1=g, op0=ALU.mult, op1=ALU.add)
                    ins.then_inc(S["ffn_r"], 1)

            def second_residual(u):
                for t in range(TPU):
                    n = TPU * u + t
                    x3 = xr[u % XS][:, t, :]
                    dve.wait_ge(S["o2_mm"], n + 1)
                    dve.wait_ge(S["xh2_r"], n + 1)
                    dve.tensor_tensor(x3, x3, PS[:, 6 + t, :], ALU.add).then_inc(S["x3_r"], 1)

            dve.wait_ge(S["y_ev"], NG)
            y_stats(0, range(TPS))
            y_stats(1, range(TPS))
            for u in range(NU + 2):
                if u < NU:
                    first_residual(u, 0)
                    v, h = u // 2 + 2, u % 2
                    if v < NT:
                        y_stats(v, range(TPU * h, TPU * h + TPU))
                    first_residual(u, 1)
                if 1 <= u <= NU:
                    ffn(u - 1)
                if u >= 2:
                    second_residual(u - 2)

        @block.tensor
        def _(pe):
            pe.wait_ge(S["ident_r"], 1)
            pe.wait_ge(S["ld_bc"], 32)
            pe.transpose(PS[:, 7, 0:128], bcn, ident[:, :]).then_inc(S["bct_mm"], 1)
            pe.wait_ge(S["crep_r"], 1)
            pe.wait_ge(S["bct_ev"], 1)

            def mod_row(i):
                j = MOD_ORDER[i]
                pe.wait_ge(ld_wm[j], 16)
                w = wm_first[:, i, :, :] if i < 2 else wm_later
                if j in (3, 4):
                    for q in range(QB):
                        for k in range(QB):
                            mm = pe.matmul(PS[:, 6 + i % 2, q:q + 1], w[:, k, q * P:(q + 1) * P], ccol[:, k:k + 1],
                                           start=(k == 0), stop=(k == QB - 1))
                else:
                    for k in range(QB):
                        mm = pe.matmul(PS[:, 6 + i % 2, :], crep[:, k, :], w[:, k, :], start=(k == 0), stop=(k == QB - 1))
                mm.then_inc(S["mod_mm"], 1)

            mod_row(0)
            mod_row(1)

            for half in range(HALVES):
                base = half * HSTEPS
                pe.wait_ge(S["v0_r"], 2 * (half + 1))
                if half:
                    pe.wait_ge(S["y_ev"], half * HG)
                for n in range(STEPS):
                    k, o, r, w = n // OCT, n % OCT, (base + n) % 2, 2 ** (n // OCT)
                    b = (base + n) % BDR
                    pe.wait_ge(S["bdt_r"], base + n + 1)
                    if base + n >= 2:
                        pe.wait_ge(S["lvl_ev"], base + n - 1)
                    for j in range(8):
                        g = 8 * o + j
                        for e in QD:
                            pe.matmul(pv_ps(r)[e:e + 32, j, 0:w + NS], BDTs[e:e + 32, b, j, :], PV[e:e + 32, g, PW - w:PW + NS],
                                      start=True, stop=True)
                        for e in QD:
                            mm = pe.matmul(w_ps(r)[e:e + 32, j, 0:w], BDs[e:e + 32, b, j, :], WP[e:e + 32, g, L + 1 - w:L + 1],
                                           start=True, stop=True)
                    mm.then_inc(S["lvl_mm"], 1)
                pe.wait_ge(S["lvl_ev"], base + STEPS)
                pe.wait_ge(S["cm_r"], half + 1)
                for g in range(HG):
                    mm = pe.matmul(PS[:, 6, g * GC:(g + 1) * GC], PV[:, g, 0:L], CM[:, g, :], start=True, stop=True)
                mm.then_inc(S["k_mm"], 1)
                pe.wait_ge(S["k_sb"], half + 1)
                for b in range(2):
                    mm = pe.transpose(PS[:, 7, b * P:(b + 1) * P], ksb[:, b * P:(b + 1) * P], ident[:, :])
                mm.then_inc(S["kt_mm"], 1)
                pe.wait_ge(S["kt_r"], half + 1)

                def input_mats(q):
                    n = 8 * half + q
                    if q >= 2:
                        pe.wait_ge(S["ut_ev"], n - 1)
                    for i in range(4):
                        mm = pe.transpose(PS[:, 6 + q % 2, i * P:(i + 1) * P], PV[:, 4 * q + i, 0:L], ident[:, :])
                    mm.then_inc(S["ut_mm"], 1)

                if half == 0:
                    pe.wait_ge(S["xy_r"], NC)
                input_mats(0)
                for q in range(8):
                    n = 8 * half + q
                    if q < 7:
                        input_mats(q + 1)
                    pe.wait_ge(S["ut_ev"], n + 1)
                    if q >= 4:
                        pe.wait_ge(S["u_ev"], n - 3)
                    for i in range(4):
                        for e in range(4):
                            d = (half * HG + 4 * q + i) * GC + 2 * e
                            mm = pe.matmul(PS[32 * e:32 * e + 32, q % 4, i * P:(i + 1) * P],
                                           Uring[:, q % 2, i * P + 32 * e:i * P + 32 * e + 32], XY[:, d:d + 2, :],
                                           start=True, stop=True)
                    mm.then_inc(S["u_mm"], 1)
                pe.wait_ge(S["u_ev"], 8 * (half + 1))
                for i in range(SSTEPS):
                    k, o, n = i // OCT, i % OCT, base + STEPS + i
                    r, b = n % 2, n % BDR
                    pe.wait_ge(S["bdt_r"], n + 1)
                    if i >= 2:
                        pe.wait_ge(S["scan_h"], half * SSTEPS + i - 1)
                    for j in range(8):
                        g = 8 * o + j
                        for e in QD:
                            mm = pe.matmul(pv_ps(r)[e:e + 32, j, 0:NS + NC], BDTs[e:e + 32, b, j, :], PV[e:e + 32, g, H0:PW + NS],
                                           start=True, stop=True)
                        if k == 0:
                            for e in QD:
                                mm = pe.matmul(w_ps(r)[e:e + 32, j, 0:1], BDs[e:e + 32, b, j, :], WP[e:e + 32, g, L:L + 1],
                                               start=True, stop=True)
                    mm.then_inc(S["lvl_mm"], 1)
                    if half == 0 and i % MODE == MODE - 1 and i // MODE < 4:
                        mod_row(2 + i // MODE)
                pe.wait_ge(S["scan_h"], (half + 1) * SSTEPS)
                if half == HALVES - 1:
                    pe.wait_ge(S["ld_wo"], 16)
                    for q in range(QB):
                        if q >= 2:
                            pe.wait_ge(S["wo_ev"], q - 1)
                        for o in range(QB):
                            mm = pe.transpose(PS[:, 6 + q % 2, o * P:(o + 1) * P], WoN[:, o, q * P:(q + 1) * P], ident[:, :])
                        mm.then_inc(S["wo_tr"], 1)
                for g in range(HG):
                    n = half * HG + g
                    if half == HALVES - 1 and g == HG // 2:
                        pe.wait_ge(S["ld_w"], 16 * 15)
                        for r in range(2):
                            for q in range(QB):
                                mm = pe.matmul(PS[64 * r:64 * r + 64, 5, 0:1], WinS[:, q, :], cbsb[:, 4 + q:5 + q], start=(q == 0), stop=(q == QB - 1))
                        mm.then_inc(S["prep_mm"], 1)
                    if g >= 4:
                        pe.wait_ge(S["y_ev"], n - 3)
                    pe.wait_ge(S["bdh_r"], n + 1)
                    if g == 0:
                        pe.wait_ge(S["bz_r"], half + 1)
                    pe.matmul(PS[:, g % 4, :], WP[:, g, 0:L], BDH[:, g % 2, :, :], start=True, stop=False,
                              skip_group_check=True).then_inc(S["o_mm"], 1)
                    pe.wait_ge(t_ld[n % 3], 16 * (n // 3 + 1))
                    for h in range(GC):
                        mm = pe.matmul(PS[:, g % 4, h * NC:(h + 1) * NC], Tring[:, n % 3, h, :], XY[:, n * GC + h, :],
                                       start=False, stop=(h == GC - 1), skip_group_check=True)
                    mm.then_inc(S["t_mm"], 1)

            pe.wait_ge(S["wo_ev"], QB)
            pe.wait_ge(S["y_ev"], NG)
            pe.wait_ge(S["prep_r"], 2)

            def t_y(u, b):
                pe.wait_ge(S["yh_r"], TPU * (u + 1))
                if u >= 1:
                    pe.wait_ge(S["gelu_r"], QB * (u - 1) + 2 * (b + 1))
                for q in (2 * b, 2 * b + 1):
                    for t in range(TPU):
                        i = (q % 2) * UW + t * P
                        mm = pe.transpose(PS[:, b, i:i + P], hatY[:, u % 2, t, q * P:(q + 1) * P], ident[:, :])
                mm.then_inc(S["ty_mm"], 1)

            def out1(u, t, qs):
                n = TPU * u + t
                if qs[0] == 0:
                    pe.wait_ge(S["gelu_r"], QB * (u + 1))
                    if u >= 1:
                        pe.wait_ge(S["x2_r"], n - TPU + 1)
                for q in qs:
                    pe.matmul(PS[:, 2 + t, :], zT[:, u % 2, q, t * P:(t + 1) * P], WoT[:, q, :], start=(q == 0), stop=False)
                if qs[-1] == QB - 1:
                    pe.matmul(PS[:, 2 + t, :], ones_bf[0:3, :], bias1[0:3, :], start=False, stop=True).then_inc(S["o1_mm"], 1)

            def t_x(u, b):
                pe.wait_ge(S["xh2_r"], TPU * (u + 1))
                if 2 * u + b >= 1:
                    pe.wait_ge(S["xT_r"], 2 * u + b)
                for q in (2 * b, 2 * b + 1):
                    for t in range(TPU):
                        i = (q % 2) * UW + t * P
                        mm = pe.transpose(PS[:, 4, i:i + P], hatX[:, u % 2, t, q * P:(q + 1) * P], ident[:, :])
                mm.then_inc(S["tx_mm"], 1)

            def s_prod(u):
                pe.wait_ge(S["xT_r"], 2 * (u + 1))
                if u >= 1:
                    pe.wait_ge(S["relu_r"], INNER * u)
                for q in range(QB):
                    for t in range(TPU):
                        mm = pe.matmul(PS[M * t:M * t + M, 5, 0:P], WinS[:, q, :], x2T[:, u % 2, q, t * P:(t + 1) * P],
                                       start=(q == 0), stop=(q == QB - 1))
                mm.then_inc(S["s_mm"], 1)

            def out2(u):
                pe.wait_ge(S["ffn_r"], INNER * (u + 1))
                if u >= 1:
                    pe.wait_ge(S["x3_r"], TPU * u)
                for t in range(TPU):
                    pe.matmul(PS[:, 6 + t, :], gS[M * t:M * t + M, u % 2, :], WoutS[M * t:M * t + M, :], start=True, stop=False)
                for t in range(TPU):
                    pe.matmul(PS[:, 6 + t, :], ones_bf[0:3, :], bias2[0:3, :], start=False, stop=True).then_inc(S["o2_mm"], 1)

            t_y(0, 0)
            t_y(0, 1)
            for u in range(NU + 2):
                if u < NU:
                    out1(u, 0, (0, 1, 2, 3))
                if u + 1 < NU:
                    t_y(u + 1, 0)
                    t_y(u + 1, 1)
                if 1 <= u <= NU:
                    t_x(u - 1, 0)
                if u < NU:
                    out1(u, 1, (0, 1))
                if 1 <= u <= NU:
                    t_x(u - 1, 1)
                if u < NU:
                    out1(u, 1, (2, 3))
                if 1 <= u <= NU:
                    s_prod(u - 1)
                if u >= 2:
                    out2(u - 2)


def scan_add(dve, S, PV, pv_ps, half, base, i, ALU):
    k, o, n = i // OCT, i % OCT, base + STEPS + i
    w = 2 ** k
    dve.wait_ge(S["lvl_ev"], n + 1)
    st = PV[:, 8 * o:8 * o + 8, H0 + w:H0 + NC]
    dve.tensor_tensor(st, st, pv_ps(n % 2)[:, :, 0:NC - w], ALU.add).then_inc(S["scan_h"], 1)


_INS = ['L0_attn_x', 'L0_attn_A', 'L0_attn_Bm', 'L0_attn_Cm', 'L0_attn_Dm', 'L0_attn_ln_w', 'L0_attn_ln_b',
        'L0_attn_W_out', 'L0_attn_b_out', 'L0_ffn_Win', 'L0_ffn_bin_', 'L0_ffn_W1', 'L0_ffn_b1', 'L0_ffn_W2',
        'L0_ffn_b2', 'L0_ffn_Wout', 'L0_ffn_bout', 'L0_c', 'L0_wmod']


def kernel(**inputs):
    import numpy as _np
    import concourse.bacc as _bacc
    from concourse import mybir as _mybir
    from concourse.bass_utils import run_bass_kernel_spmd as _run

    nc = _bacc.Bacc("TRN2", target_bir_lowering=False, num_devices=1)
    arrays, args = {}, []
    for name in _INS:
        a = _np.ascontiguousarray(inputs[name])
        arrays[f"in_{name}"] = a
        args.append(nc.dram_tensor(f"in_{name}", a.shape, _mybir.dt.from_np(a.dtype), kind="ExternalInput").ap())
    res = nc.dram_tensor("out_0", (1, T, D), _mybir.dt.float32, kind="ExternalOutput").ap()
    adaln_ssm_kernel(nc, *args, res)
    r = _run(nc, [arrays], core_ids=[0])
    return r.results[0]["out_0"]
```

```python
import numpy as np
import concourse.bass as bass
from concourse import mybir
from contextlib import ExitStack


P = 128
D = 512
T = 8192
NS = 16
L = P
NC = T // L
GC = P // NS
NG = D // GC
HALVES = 2
HG = NG // HALVES
HD = D // HALVES
OCT = HG // 8
LEVELS = 7
PW = L
H0 = L - NC
SCANS = 6
STEPS = LEVELS * OCT
SSTEPS = SCANS * OCT
HSTEPS = STEPS + SSTEPS
QB = D // P
M = 64
INNER = 16
EPS = 1e-5
TPS = 4
NT = NC // TPS
TPU = 2
NU = NC // TPU
UW = TPU * P
XS = 8
FP = 2
LAG = 4
RELU_RING = 4
XR = 10
LNB = 4
LNA = 7
MODE = 4
BDR = 4
QD = range(0, P, 2 * NS)


def adaln_ssm_kernel(nc, x_in, A_in, Bm_in, Cm_in, Dm_in, lnw_in, lnb_in, Wo_in, bo_in,
                     Win_in, bin_in, W1_in, b1_in, W2_in, b2_in, Wout_in, bout_in, c_in, wmod_in, out):
    f32 = mybir.dt.float32
    bf16 = mybir.dt.bfloat16
    ALU = mybir.AluOpType
    ACT = mybir.ActivationFunctionType
    AX = mybir.AxisListType

    kscr = nc.dram_tensor("kernel_taps", [D, 2 * L], f32, kind="Internal").ap()
    x_t = x_in[0].rearrange("(c p) d -> p c d", p=P)
    out_t = out[0].rearrange("(c p) d -> p c d", p=P)

    ctx = ExitStack()
    with ctx:
        def sb(name, shape, dt=f32):
            return ctx.enter_context(nc.sbuf_tensor(name, shape, dt))

        def sem(name):
            return ctx.enter_context(nc.semaphore(name))

        XY = sb("XY", [P, D, NC])
        A0 = sb("arenaA", [P, 8736])
        PV = A0[:, 0:HG * 144].rearrange("p (g w) -> p g w", w=144)
        WP = A0[:, 4608:4608 + HG * 129].rearrange("p (g w) -> p g w", w=129)
        C0 = sb("arenaC", [P, 8192])
        BDs = C0[:, 0:1024].rearrange("p (r g m) -> p r g m", r=BDR, g=8)
        BDTs = C0[:, 1024:2048].rearrange("p (r g m) -> p r g m", r=BDR, g=8)
        UR = C0[:, 2048:3072]
        BDF = C0[:, 6144:8192].rearrange("p (r g m) -> p r g m", r=2, g=8)
        ROWS = sb("ROWS", [P, 4, D])
        ident = sb("ident", [P, P])
        bcs = sb("bcs", [P, 256])
        mask8 = sb("mask8", [P, GC])
        par = sb("par", [P, 2])
        ST = sb("ST", [P, 3, NC])
        ccol = sb("ccol", [P, QB])
        DmT = sb("DmT", [P, QB])
        cbsb = sb("cbsb", [P, 2 * QB])
        lnwb = sb("lnwb", [P, 2 * QB])
        bs6 = sb("bs6", [P, 4, 6])
        half_neg = sb("half_neg", [P, 8])

        CA1, SA, GA, GB = (ROWS[:, i, :] for i in range(4))
        mean_x, rstd_x, nmr_x = (ST[:, i, :] for i in range(3))
        wm_first = XY[:, 0:2 * 4 * 8, :].rearrange("p (j k r) c -> p j k (r c)", j=2, k=4)
        wm_later = C0[:, 6144:8192].rearrange("p (k n) -> p k n", k=QB)
        crep = GB.rearrange("p (k m) -> p k m", k=4)
        bcn = bcs[:, 0:128]
        BCT = bcs[:, 128:256]
        CM = UR.rearrange("p (g c) -> p g c", c=4 * GC)
        Uring = C0[:, 3072:4096].rearrange("p (r w) -> p r w", r=2)
        ktz = C0[:, 4096:4608].rearrange("p (b w) -> p b w", b=2)
        BDH = UR.rearrange("p (r h c) -> p r h c", r=2, h=GC)
        Tring = C0[:, 3072:6144].rearrange("p (r h i) -> p r h i", r=3, h=GC)
        xst = C0[:, 3072:3072 + XR * D].rearrange("p (r d) -> p r d", r=XR)
        zT = A0[:, 0:2048].rearrange("p (r q t) -> p r q t", r=2, q=QB)
        x2T = A0[:, 2048:3072].rearrange("p (q t) -> p q t", q=QB)
        hatX = A0[:, 3072:4096].rearrange("p (t d) -> p t d", t=TPU)
        rr = A0[:, 4096:5120].rearrange("p (r t) -> p r t", r=RELU_RING)
        gS = GA.rearrange("p (r t) -> p r t", r=2)
        hatY = C0[:, 0:1024].rearrange("p (t d) -> p t d", t=TPU)
        xr = [C0[:, 1024 * i:1024 * (i + 1)].rearrange("p (t d) -> p t d", t=TPU) for i in range(1, 6)]
        xr += [A0[:, 1024 * i:1024 * (i + 1)].rearrange("p (t d) -> p t d", t=TPU) for i in range(5, 8)]
        WoN = C0[:, 0:2048].rearrange("p (o d) -> p o d", o=QB)
        WoT = C0[:, 6144:8192].rearrange("p (q d) -> p q d", q=QB)
        Grow = CA1
        tmp = SA
        b1row, b2row = C0[:, 0:512], C0[:, 512:1024]
        part = C0[:, 1024:1280].bitcast(bf16)
        WoutN = C0[:, 1280:1792]
        WoutS = GB
        WinS = sb("WinS", [P, QB, M])
        bias1 = sb("bias1", [P, D], bf16)
        bias2 = bcs[:, 0:256].bitcast(bf16)
        ones_bf = sb("ones_bf", [P, P], bf16)
        ffc = sb("ffc", [P, 3 * INNER + 4])
        W1c, b1c, W2c = (ffc[:, i * INNER:(i + 1) * INNER] for i in range(3))
        b2c, binc = ffc[:, 48:49], ffc[:, 49:50]
        bx6 = sb("bx6", [P, TPU, 6])
        mvy = sb("mvy", [P, TPS, 2])
        mvx = sb("mvx", [P, 2, TPU, 2])
        sy = sb("sy", [P, 2, 2, TPS])
        s2 = sb("s2", [P, 2, 2, TPU])

        PS = ctx.enter_context(nc.psum_tensor("PS", [P, 8, 512], f32))

        def pv_ps(r):
            return PS[:, 2 * r:2 * r + 2, :].rearrange("p b (s w) -> p (b s) w", w=128)

        def w_ps(r):
            return PS[:, 4 + r, :].rearrange("p (g w) -> p g w", w=64)

        S = {}
        for name in ("consts", "ident_r", "ld_c", "ld_bc", "ld_A", "ld_small", "silu_r", "crep_r", "mod_mm", "mod_ev",
                     "bct_mm", "bct_ev", "par_r", "v0_r",
                     "bn_r", "rst_r", "xh_r", "xm_r", "xy_r", "dchain", "pchain",
                     "bd_r", "bdt_r", "lvl_mm", "lvl_ev", "scan_h", "cm_r", "kz_r", "k_mm", "w128_mm", "w128_ev", "kt_r", "bdf_z", "bdf_r", "k_saved",
                     "ut_mm", "ut_ev", "u_mm", "u_ev", "bdh_r", "o_mm", "t_mm", "y_ev", "bz_r",
                     "ld_wo", "wo_tr", "wo_ev", "ld_w", "prep_r", "prep_mm",
                     "ty_mm", "gelu_r", "o1_mm", "x2_r", "yst", "yr_r", "yh_r", "x2st", "x2rs", "xh2_r", "tx_mm", "xT_r",
                     "s_mm", "relu_r", "ffn_r", "o2_mm", "x3_r", "xres_r"):
            S[name] = sem(name)
        ld_wm = [sem(f"ld_wm{j}") for j in range(6)]
        x_ld = [sem(f"x_ld{r}") for r in range(XR)]
        t_ld = [sem(f"t_ld{r}") for r in range(3)]
        xc_ld = [sem(f"xc_ld{r}") for r in range(XS)]
        x_st = [sem(f"x_st{r}") for r in range(XS)]

        MOD_ORDER = [1, 0, 4, 3, 2, 5]

        H_A, H_B = range(INNER // 2), range(INNER // 2, INNER)

        def tiles_of(n):
            return range(NC * n // STEPS, NC * (n + 1) // STEPS)

        block = ctx.enter_context(nc.Block())

        @block.sync
        def _(sp):
            with nc.allow_non_contiguous_dma(reason="columns of a few hundred elements"):
                sp.dma_start(ccol[:, :], c_in[0].rearrange("(k p) -> p k", p=P)).then_inc(S["ld_c"], 16)
                sp.dma_start(bcn[0:64, :], Bm_in.rearrange("(g c) n -> g (c n)", c=GC)).then_inc(S["ld_bc"], 16)
                sp.dma_start(bcn[64:128, :], Cm_in.rearrange("(g c) n -> g (c n)", c=GC)).then_inc(S["ld_bc"], 16)
                wv = wmod_in.rearrange("(k p) n -> p k n", p=P)
                for i in range(2):
                    j = MOD_ORDER[i]
                    sp.dma_start(wm_first[:, i, :, :], wv[:, :, j * D:(j + 1) * D]).then_inc(ld_wm[j], 16)
            Av = A_in.rearrange("(g c) n m -> (c n) g m", c=GC)

            def load_A(half):
                sp.dma_start(PV[:, :, PW:PW + NS], Av[:, half * HG:(half + 1) * HG, :]).then_inc(S["ld_A"], 16)

            load_A(0)
            with nc.allow_non_contiguous_dma(reason="columns of a few hundred elements"):
                sp.dma_start(DmT[:, :], Dm_in.rearrange("(k p) -> p k", p=P)).then_inc(S["ld_small"], 16)
                sp.dma_start(lnwb[:, 0:QB], lnw_in.rearrange("(k p) -> p k", p=P)).then_inc(S["ld_small"], 16)
                sp.dma_start(lnwb[:, QB:], lnb_in.rearrange("(k p) -> p k", p=P)).then_inc(S["ld_small"], 16)

            def load_x(c):
                if c >= XR:
                    sp.wait_ge(S["xh_r"], c - XR + 1)
                sp.dma_start(xst[:, c % XR, :], x_t[:, c, :]).then_inc(x_ld[c % XR], 16)

            for c in range(NC):
                load_x(c)
            def load_last_weights(g):
                with nc.allow_non_contiguous_dma(reason="columns of a few hundred elements"):
                    if g == 1:
                        sp.wait_ge(S["lvl_mm"], HALVES * HSTEPS)
                        sp.dma_start(WoN, Wo_in.rearrange("(o p) d -> p o d", p=P)).then_inc(S["ld_wo"], 16)
                    if g == 4:
                        sp.dma_start(WinS[:, :, :], Win_in.rearrange("(q p) m -> p q m", p=P)).then_inc(S["ld_w"], 16)
                    if g in (5, 6):
                        rows = slice(64 * (g - 5), 64 * (g - 4))
                        for dst, src in ((W1c, W1_in), (b1c, b1_in), (W2c, W2_in)):
                            sp.dma_start(dst[rows, :], src).then_inc(S["ld_w"], 16)
                    if g in (7, 8):
                        rows = slice(64 * (g - 7), 64 * (g - 6))
                        sp.dma_start(b2c[rows, :], b2_in.rearrange("(m a) -> m a", a=1)).then_inc(S["ld_w"], 16)
                        sp.dma_start(binc[rows, :], bin_in.rearrange("(m a) -> m a", a=1)).then_inc(S["ld_w"], 16)
                    if g == 12:
                        sp.wait_ge(S["wo_tr"], QB)
                        sp.dma_start(b1row, bo_in.partition_broadcast(P)).then_inc(S["ld_w"], 16)
                        sp.dma_start(b2row, bout_in.partition_broadcast(P)).then_inc(S["ld_w"], 16)
                    if g in (13, 14):
                        sp.dma_start(WoutN[64 * (g - 13):64 * (g - 12), :], Wout_in).then_inc(S["ld_w"], 16)

            for half in range(HALVES):
                if half:
                    sp.wait_ge(S["o_mm"], half * HG)
                    sp.wait_ge(S["bdh_r"], half * HG)
                    load_A(half)
                sp.wait_ge(S["kt_r"], half + 1)
                sp.dma_start(kscr[half * HD:(half + 1) * HD, :].rearrange("(b p) w -> p b w", p=P), ktz).then_inc(S["k_saved"], 16)
                sp.wait_ge(S["k_saved"], 16 * (half + 1))
                sp.wait_ge(S["u_mm"], 8 * (half + 1))
                for g in range(HG):
                    n = half * HG + g
                    if n >= 3:
                        sp.wait_ge(S["t_mm"], n - 2)
                    row = (half * HG + g) * GC
                    src = bass.AP(kscr.tensor, row * 2 * L, [[1, P], [2 * L, GC], [1, L]])
                    sp.dma_start(Tring[:, n % 3, :, :], src).then_inc(t_ld[n % 3], 16)
                    if half == 0 and g % MODE == MODE - 1 and g // MODE in (0, 2, 3, 4):
                        i = 2 + max(g // MODE - 1, 0)
                        if i == 2:
                            sp.wait_ge(S["lvl_mm"], HSTEPS)
                        else:
                            sp.wait_ge(S["mod_mm"], i)
                        j = MOD_ORDER[i]
                        sp.dma_start(wm_later, wv[:, :, j * D:(j + 1) * D]).then_inc(ld_wm[j], 16)
                    if half == HALVES - 1:
                        load_last_weights(g)
            sp.wait_ge(S["t_mm"], NG)
            sp.wait_ge(S["bdh_r"], NG)

            def load_unit(u):
                sp.dma_start(xr[u % XS], x_t[:, u * TPU:(u + 1) * TPU, :]).then_inc(xc_ld[u % XS], 16)

            for u in range(XS):
                if u == 0:
                    sp.wait_ge(S["prep_r"], 2)
                load_unit(u)
            for u in range(NU):
                b = u % XS
                sp.wait_ge(S["x3_r"], TPU * (u + 1))
                sp.dma_start(out_t[:, u * TPU:(u + 1) * TPU, :], xr[b]).then_inc(x_st[b], 16)
                if u + XS < NU:
                    sp.wait_ge(x_st[b], 16 * (u // XS + 1))
                    load_unit(u + XS)
            for b in range(XS):
                sp.wait_ge(x_st[b], 16 * ((NU - 1 - b) // XS + 1))

        @block.gpsimd
        def _(gp):
            nch = [0]

            def chain(ins):
                nch[0] += 1
                ins.then_inc(S["pchain"], 1)
                gp.wait_ge(S["pchain"], nch[0])

            chain(gp.memset(ident[:, :], 0.0))
            gp.affine_select(out=ident[:, :], in_=ident[:, :], compare_op=ALU.not_equal, fill=1.0, base=0,
                             pattern=[[-1, P]], channel_multiplier=1).then_inc(S["ident_r"], 1)
            gp.memset(half_neg[:, :], -0.5).then_inc(S["consts"], 1)
            gp.memset(ones_bf[:, :], 1.0).then_inc(S["consts"], 1)
            chain(gp.memset(mask8[:, :], 1.0))
            chain(gp.affine_select(out=mask8[:, :], in_=mask8[:, :], compare_op=ALU.is_ge, fill=0.0, base=0,
                                   pattern=[[-NS, GC]], channel_multiplier=1))
            gp.affine_select(out=mask8[:, :], in_=mask8[:, :], compare_op=ALU.is_ge, fill=0.0, base=NS - 1,
                             pattern=[[NS, GC]], channel_multiplier=-1).then_inc(S["consts"], 1)
            gp.wait_ge(S["consts"], 3)

            def rstd_of(var, mean, rstd, nmr, w, done):
                chain(gp.tensor_scalar(rstd, var, EPS, 0.0, ALU.add, ALU.add))
                chain(gp.tensor_tensor(rstd, rstd, half_neg[:, 0:w], ALU.pow))
                chain(gp.tensor_tensor(nmr, mean, rstd, ALU.mult))
                gp.tensor_scalar(nmr, nmr, -1.0, 0.0, ALU.mult, ALU.add).then_inc(done, 1)

            def scale_x(c):
                gp.wait_ge(S["xh_r"], c + 1)
                if c == 0:
                    gp.wait_ge(S["mod_ev"], 1)
                gp.tensor_tensor(XY[:, :, c], XY[:, :, c], CA1, ALU.mult).then_inc(S["xm_r"], 1)

            for half in range(HALVES):
                base = half * HSTEPS
                for n in range(STEPS):
                    if half == 0:
                        for c in tiles_of(n):
                            c1 = 0 if c == 0 else c + 2
                            if c1 % LNB == 0 and c1 < NC:
                                gp.wait_ge(S["bn_r"], c1 + LNB)
                                cc = slice(c1, c1 + LNB)
                                rstd_of(rstd_x[:, cc], mean_x[:, cc], rstd_x[:, cc], nmr_x[:, cc], LNB, S["rst_r"])
                            if c >= 1:
                                scale_x(c - 1)
                    if n == STEPS - 2:
                        if half == 0:
                            gp.wait_ge(S["bct_ev"], 1)
                        else:
                            gp.wait_ge(S["o_mm"], half * HG)
                        chain(gp.memset(CM, 0.0))
                        for m in range(4):
                            cb = BCT[:, 64 + half * HG + m:64 + (half + 1) * HG:4].unsqueeze(2).to_broadcast([P, HG // 4, GC])
                            gp.tensor_tensor(CM[:, m::4, GC * m:GC * m + GC], cb,
                                             mask8[:, :].unsqueeze(1).to_broadcast([P, HG // 4, GC]), ALU.mult).then_inc(S["cm_r"], 1)
                if half == 0:
                    scale_x(NC - 1)
                else:
                    gp.wait_ge(S["t_mm"], half * HG)
                gp.memset(ktz, 0.0).then_inc(S["kz_r"], 1)
                if half:
                    gp.wait_ge(S["mod_mm"], 6)
                gp.memset(BDF, 0.0).then_inc(S["bdf_z"], 1)
                gp.wait_ge(S["k_mm"], half + 1)
                gp.memset(BDH[:, :, :, 0:1], 0.0).then_inc(S["bz_r"], 1)
                for g in range(HG):
                    n = half * HG + g
                    if g % 8 == 0:
                        gp.wait_ge(S["scan_h"], half * SSTEPS + SSTEPS - OCT + g // 8 + 1)
                    if g >= 2:
                        gp.wait_ge(S["o_mm"], n - 1)
                    gp.tensor_tensor(BDH[:, g % 2, :, 1:NC], PV[:, g, H0:H0 + NC - 1].unsqueeze(1).to_broadcast([P, GC, NC - 1]),
                                     mask8[:, :].unsqueeze(2).to_broadcast([P, GC, NC - 1]), ALU.mult).then_inc(S["bdh_r"], 1)

            def rstd_y(v):
                gp.wait_ge(S["yst"], v + 1)
                if v >= 2:
                    gp.wait_ge(S["yh_r"], TPS * (v - 1))
                rstd_of(mvy[:, :, 1], mvy[:, :, 0], sy[:, v % 2, 0, :], sy[:, v % 2, 1, :], TPS, S["yr_r"])

            def residual(u):
                gp.wait_ge(xc_ld[u % XS], 16 * (u // XS + 1))
                for t in range(TPU):
                    c = TPU * u + t
                    chain(gp.tensor_scalar(tmp, xr[u % XS][:, t, :], rstd_x[:, c:c + 1], nmr_x[:, c:c + 1], ALU.mult, ALU.add))
                    chain(gp.tensor_tensor(tmp, tmp, Grow, ALU.mult))
                    gp.tensor_tensor(xr[u % XS][:, t, :], xr[u % XS][:, t, :], tmp, ALU.add).then_inc(S["xres_r"], 1)
                    gp.wait_ge(S["xres_r"], c + 1)

            gp.wait_ge(S["prep_r"], 2)
            rstd_y(0)
            residual(0)
            rstd_y(1)
            residual(1)
            for u in range(NU):
                gp.wait_ge(S["x2st"], u + 1)
                if u >= 2:
                    gp.wait_ge(S["xh2_r"], TPU * (u - 1))
                r = u % 2
                rstd_of(mvx[:, r, :, 1], mvx[:, r, :, 0], s2[:, r, 0, :], s2[:, r, 1, :], TPU, S["x2rs"])
                if u % 2 and u // 2 + 2 < NT:
                    rstd_y(u // 2 + 2)
                if u + 2 < NU:
                    residual(u + 2)

        @block.scalar
        def _(act):
            act.wait_ge(S["ld_c"], 16)
            act.activation(ccol[:, :], ccol[:, :], ACT.Silu).then_inc(S["silu_r"], 1)
            act.wait_ge(S["bct_mm"], 1)
            act.activation(BCT, PS[:, 7, 0:128], ACT.Copy).then_inc(S["bct_ev"], 1)
            act.wait_ge(S["bct_ev"], 1)

            def normalise_x(c):
                act.wait_ge(S["rst_r"], c // LNB + 1)
                if c == 0:
                    act.wait_ge(S["mod_mm"], 2)
                act.activation(XY[:, :, c], xst[:, c % XR, :], ACT.Identity, scale=rstd_x[:, c:c + 1],
                               bias=nmr_x[:, c:c + 1]).then_inc(S["xh_r"], 1)

            for half in range(HALVES):
                base = half * HSTEPS
                if half:
                    act.wait_ge(S["o_mm"], half * HG)
                    act.wait_ge(S["bdh_r"], half * HG)
                act.activation(PV[:, :, PW - 1], BCT[:, half * HG:(half + 1) * HG], ACT.Copy).then_inc(S["v0_r"], 1)
                act.activation(WP[:, :, L], BCT[:, 64 + half * HG:64 + (half + 1) * HG], ACT.Copy).then_inc(S["v0_r"], 1)
                for c in tiles_of(0) if half == 0 else ():
                    normalise_x(c)
                for n in range(STEPS):
                    if half == 0 and n + 1 < STEPS:
                        for c in tiles_of(n + 1):
                            normalise_x(c)
                    k, o, r, w = n // OCT, n % OCT, (base + n) % 2, 2 ** (n // OCT)
                    act.wait_ge(S["lvl_mm"], base + n + 1)
                    act.activation(PV[:, 8 * o:8 * o + 8, PW:PW + NS], pv_ps(r)[:, :, w:w + NS], ACT.Copy)
                    act.activation(PV[:, 8 * o:8 * o + 8, PW - 2 * w:PW - w], pv_ps(r)[:, :, 0:w], ACT.Copy)
                    act.activation(WP[:, 8 * o:8 * o + 8, L + 1 - 2 * w:L + 1 - w], w_ps(r)[:, :, 0:w], ACT.Copy).then_inc(S["lvl_ev"], 1)
                def scan_mats(i):
                    n = base + STEPS + i
                    act.wait_ge(S["bdt_r"], n + 1)
                    act.wait_ge(S["lvl_mm"], n - 1)
                    for e in QD:
                        ins = act.activation(BDF[e:e + 32, n % 2, :, e:e + 32], BDTs[e:e + 32, n % BDR, :, :], ACT.Copy)
                    ins.then_inc(S["bdf_r"], 1)

                act.wait_ge(S["bdf_z"], half + 1)
                scan_mats(0)
                scan_mats(1)
                act.wait_ge(S["w128_mm"], half + 1)
                act.activation(WP[:, :, 0], PS[:, 5, 0:HG], ACT.Copy).then_inc(S["w128_ev"], 1)
                for q in range(8):
                    n = 8 * half + q
                    act.wait_ge(S["ut_mm"], n + 1)
                    if q >= 2:
                        act.wait_ge(S["u_mm"], n - 1)
                    elif half:
                        act.wait_ge(S["t_mm"], half * HG)
                    act.activation(Uring[:, q % 2, :], PS[:, 6 + q % 2, :], ACT.Copy).then_inc(S["ut_ev"], 1)
                for i in range(SSTEPS):
                    k, o, n = i // OCT, i % OCT, base + STEPS + i
                    r = n % 2
                    if 1 <= i < SSTEPS - 1:
                        scan_mats(i + 1)
                    act.wait_ge(S["lvl_mm"], n + 1)
                    act.activation(PV[:, 8 * o:8 * o + 8, PW:PW + NS], pv_ps(r)[:, :, NC:NC + NS], ACT.Copy).then_inc(S["lvl_ev"], 1)
                for g in range(HG):
                    n = half * HG + g
                    act.wait_ge(S["t_mm"], n + 1)
                    d = n * GC
                    act.activation(XY[:, d:d + GC, :], PS[:, g % 4, :].rearrange("p (h c) -> p h c", h=GC),
                                   ACT.Copy).then_inc(S["y_ev"], 1)

            def yhat(u):
                v = u * TPU // TPS
                act.wait_ge(S["yr_r"], v + 1)
                if u >= 1:
                    act.wait_ge(S["ty_mm"], 2 * u)
                for t in range(TPU):
                    i = (u * TPU + t) % TPS
                    act.activation(hatY[:, t, :], XY[:, :, u * TPU + t], ACT.Identity, scale=sy[:, v % 2, 0, i:i + 1],
                                   bias=sy[:, v % 2, 1, i:i + 1]).then_inc(S["yh_r"], 1)

            def gelu(u):
                if u >= 2:
                    act.wait_ge(S["o1_mm"], TPU * (u - 1))
                for q in range(QB):
                    act.wait_ge(S["ty_mm"], 2 * u + q // 2 + 1)
                    act.activation(zT[:, u % 2, q, :].rearrange("p (t i) -> p t i", i=P),
                                   PS[:, q // 2, (q % 2) * UW:(q % 2 + 1) * UW].rearrange("p (t i) -> p t i", i=P)[:, :, ::-1],
                                   ACT.Gelu, scale=lnwb[:, q:q + 1], bias=lnwb[:, QB + q:QB + q + 1]).then_inc(S["gelu_r"], 1)

            def xhat2(u):
                act.wait_ge(S["x2rs"], u + 1)
                if u >= 1:
                    act.wait_ge(S["tx_mm"], 2 * u)
                for t in range(TPU):
                    act.activation(hatX[:, t, :], xr[u % XS][:, t, :], ACT.Identity, scale=s2[:, u % 2, 0, t:t + 1],
                                   bias=s2[:, u % 2, 1, t:t + 1]).then_inc(S["xh2_r"], 1)

            def x2_columns(u, bs):
                if u >= 1:
                    act.wait_ge(S["s_mm"], u)
                for b in bs:
                    act.wait_ge(S["tx_mm"], 2 * u + b + 1)
                    act.activation(x2T[:, 2 * b:2 * b + 2, :].rearrange("p q t -> p (q t)"), PS[:, 4, :],
                                   ACT.Copy).then_inc(S["xT_r"], 1)

            def relus(p, hs):
                act.wait_ge(S["s_mm"], FP * (p + 1))
                for h in hs:
                    n = INNER * p + h
                    if n >= RELU_RING:
                        act.wait_ge(S["ffn_r"], n - RELU_RING + 1)
                    act.activation(rr[:, h % RELU_RING, :], PS[:, 5, 0:FP * P], ACT.Relu, scale=W1c[:, h:h + 1],
                                   bias=b1c[:, h:h + 1]).then_inc(S["relu_r"], 1)

            act.wait_ge(S["ld_small"], 48)
            act.wait_ge(S["prep_r"], 2)
            yhat(0)
            gelu(0)
            yhat(1)
            for u in range(NU + LAG):
                if 1 <= u <= NU:
                    xhat2(u - 1)
                if u + 1 < NU:
                    gelu(u + 1)
                if u % 2 and 3 <= u <= NU + 1:
                    relus((u - 3) // 2, H_B[:3])
                if 1 <= u <= NU:
                    x2_columns(u - 1, (0,))
                if u % 2 and 3 <= u <= NU + 1:
                    relus((u - 3) // 2, H_B[3:])
                if 1 <= u <= NU:
                    x2_columns(u - 1, (1,))
                if u + 2 < NU:
                    yhat(u + 2)
                if u % 2 == 0 and 2 <= u <= NU:
                    relus((u - 2) // 2, H_A)

        @block.vector
        def _(dve):
            nch = [0]

            def chain(ins):
                nch[0] += 1
                ins.then_inc(S["dchain"], 1)
                dve.wait_ge(S["dchain"], nch[0])

            dve.wait_ge(S["silu_r"], 1)
            dve.tensor_copy(crep, ccol[:, :].unsqueeze(2).to_broadcast([P, QB, P])).then_inc(S["crep_r"], 1)
            dve.wait_ge(S["consts"], 3)
            for e in range(2):
                dve.reduce_sum(par[:, e:e + 1], mask8[:, e::2], AX.X).then_inc(S["par_r"], 1)
            dve.wait_ge(S["par_r"], 2)

            def mod_rows(which):
                for i in which:
                    j = MOD_ORDER[i]
                    dve.wait_ge(S["mod_mm"], i + 1)
                    src, sgn = PS[:, 6 + i % 2, :], PS[:, 7 - i % 2, :]
                    if j == 1:
                        dve.tensor_scalar(CA1, src, 1.0, None, ALU.add).then_inc(S["mod_ev"], 1)
                    elif j == 0:
                        dve.tensor_copy(SA, src).then_inc(S["mod_ev"], 1)
                    elif j in (2, 5):
                        row = GA if j == 2 else GB
                        dve.tensor_scalar(sgn, src, 0.0, 2.0, ALU.is_ge, ALU.mult)
                        chain(dve.tensor_scalar(row, src, -1.0, 0.25, ALU.mult, ALU.max))
                        chain(dve.tensor_tensor(row, row, src, ALU.max))
                        ins = dve.scalar_tensor_tensor(out=row, in0=sgn, scalar=-1.0, in1=row, op0=ALU.add, op1=ALU.mult)
                        ins.then_inc(S["mod_ev"], 1)
                        dve.wait_ge(S["mod_ev"], i + 1)
                    else:
                        dst = cbsb[:, 0:QB] if j == 4 else cbsb[:, QB:]
                        diag = GA.rearrange("p (q m) -> p q m", q=QB)
                        chain(dve.tensor_tensor(diag, src.rearrange("p (q m) -> p q m", q=QB),
                                                ident[:, :].unsqueeze(1).to_broadcast([P, QB, P]), ALU.mult))
                        ins = dve.reduce_sum(dst, diag, AX.X)
                        if j == 4:
                            chain(ins)
                            ins = dve.tensor_scalar(dst, dst, 1.0, None, ALU.add)
                        ins.then_inc(S["mod_ev"], 1)
                        dve.wait_ge(S["mod_ev"], i + 1)

            def stats_x(c):
                dve.wait_ge(x_ld[c % XR], 16 * (c // XR + 1))
                if c >= 4:
                    dve.wait_ge(S["bn_r"], c - 3)
                chain(dve.bn_stats(bs6[:, c % 4, :], xst[:, c % XR, :]))
                dve.bn_aggr(ST[:, 0:2, c], bs6[:, c % 4, :]).then_inc(S["bn_r"], 1)

            def shift_x(c):
                dve.wait_ge(S["xm_r"], c + 1)
                dve.tensor_tensor(XY[:, :, c], XY[:, :, c], SA, ALU.add).then_inc(S["xy_r"], 1)

            def power_mats(half, k, o, n):
                if k == 0:
                    if o == 0:
                        dve.wait_ge(S["ld_A"], 16 * (half + 1))
                else:
                    dve.wait_ge(S["lvl_ev"], n - OCT + 1)
                if n >= BDR:
                    dve.wait_ge(S["lvl_mm"], n - BDR + 1)
                src = PV[:, 8 * o:8 * o + 8, PW:PW + NS].unsqueeze(2).to_broadcast([P, 8, 2, NS])
                msk = par[:, :].unsqueeze(1).unsqueeze(3).to_broadcast([P, 8, 2, NS])
                dve.tensor_tensor(BDs[:, n % BDR, :, :].rearrange("p g (a m) -> p g a m", m=NS), src, msk,
                                  ALU.mult).then_inc(S["bd_r"], 1)
                dve.wait_ge(S["bd_r"], n + 1)
                dve.transpose(BDTs[:, n % BDR, :, :], BDs[:, n % BDR, :, :]).then_inc(S["bdt_r"], 1)

            for half in range(HALVES):
                base = half * HSTEPS
                for n in range(STEPS):
                    if n == 0 and half == 0:
                        for c in range(LNA):
                            stats_x(c)
                        mod_rows(range(2))
                    power_mats(half, n // OCT, n % OCT, base + n)
                    if half == 0:
                        for c in tiles_of(n):
                            if c + LNA < NC:
                                stats_x(c + LNA)
                            if c >= 2:
                                shift_x(c - 2)
                if half == 0:
                    for c in (NC - 2, NC - 1):
                        shift_x(c)
                for i in range(OCT):
                    power_mats(half, LEVELS, i, base + STEPS + i)
                dve.wait_ge(S["k_mm"], half + 1)
                dve.wait_ge(S["kz_r"], half + 1)
                if half == 0:
                    dve.wait_ge(S["ld_small"], 48)
                chain(dve.tensor_copy(ktz[:, :, 0:L], PS[:, 4, 0:HD].rearrange("p (b w) -> p b w", b=2)))
                dve.tensor_tensor(ktz[:, :, L - 1], ktz[:, :, L - 1], DmT[:, 2 * half:2 * half + 2], ALU.add).then_inc(S["kt_r"], 1)
                for q in range(8):
                    n = 8 * half + q
                    dve.wait_ge(S["u_mm"], n + 1)
                    ps = PS[:, q % 4, :].rearrange("p (g a c) -> p g a c", g=4, a=2)
                    st = PV[:, 4 * q:4 * q + 4, H0:H0 + NC]
                    chain(dve.tensor_scalar(st, ps[:, :, 0, :], par[:, 0:1], None, ALU.mult))
                    dve.scalar_tensor_tensor(out=st, in0=ps[:, :, 1, :], scalar=par[:, 1:2], in1=st, op0=ALU.mult,
                                             op1=ALU.add).then_inc(S["u_ev"], 1)
                dve.wait_ge(S["u_ev"], 8 * (half + 1))
                for i in range(SSTEPS):
                    k, o, n = i // OCT, i % OCT, base + STEPS + i
                    if OCT <= i + 2 < SSTEPS:
                        power_mats(half, LEVELS + (i + 2) // OCT, (i + 2) % OCT, n + 2)
                    if i >= 1:
                        scan_add(dve, S, PV, pv_ps, half, base, i - 1, ALU)
                scan_add(dve, S, PV, pv_ps, half, base, SSTEPS - 1, ALU)
                if half == 0:
                    mod_rows(range(2, 6))

            for q in range(QB):
                dve.wait_ge(S["wo_tr"], q + 1)
                dve.tensor_tensor(WoT[:, q, :], PS[:, 6 + q % 2, :], GA, ALU.mult).then_inc(S["wo_ev"], 1)

            dve.wait_ge(S["ld_w"], 16 * 15)
            dve.wait_ge(S["prep_mm"], 1)
            dve.tensor_tensor(binc, binc, PS[:, 5, 0:1], ALU.add).then_inc(S["dchain"], 1)
            for q in range(QB):
                dve.tensor_scalar(WinS[:, q, :], WinS[:, q, :], cbsb[:, q:q + 1], None, ALU.mult).then_inc(S["dchain"], 1)
            dve.tensor_tensor(b1row, b1row, SA, ALU.add).then_inc(S["dchain"], 1)
            dve.tensor_tensor(b2row, b2row, GB, ALU.mult).then_inc(S["dchain"], 1)
            dve.tensor_tensor(Grow, CA1, GA, ALU.mult).then_inc(S["dchain"], 1)
            nch[0] += 1 + QB + 3
            dve.wait_ge(S["dchain"], nch[0])
            chain(dve.scalar_tensor_tensor(out=b1c, in0=W1c, scalar=binc, in1=b1c, op0=ALU.mult, op1=ALU.add))
            chain(dve.tensor_tensor(WoutS, WoutN, GB, ALU.mult))
            chain(dve.tensor_tensor(b1row, b1row, GA, ALU.mult))
            up, acc = PS[:, 7, :], tmp
            for rest, dst in ((b1row, bias1[:, :]), (b2row, bias2)):
                for i in range(3):
                    chain(dve.tensor_copy(part, rest))
                    chain(dve.tensor_copy(up, part))
                    if i == 0:
                        chain(dve.tensor_scalar(acc, up, ident[:, i:i + 1], None, ALU.mult))
                    else:
                        chain(dve.scalar_tensor_tensor(out=acc, in0=up, scalar=ident[:, i:i + 1], in1=acc, op0=ALU.mult, op1=ALU.add))
                    chain(dve.tensor_tensor(rest, rest, up, ALU.subtract))
                chain(dve.tensor_copy(dst, acc))
            dve.memset(bs6[:, 0, 0:1], 0.0).then_inc(S["prep_r"], 2)
            dve.wait_ge(S["prep_r"], 2)

            def y_stats(v, ts):
                if v >= 1 and ts[0] == 0:
                    dve.wait_ge(S["yst"], v)
                for t in ts:
                    dve.bn_stats(bs6[:, t, :], XY[:, :, v * TPS + t]).then_inc(S["dchain"], 1)
                nch[0] += len(ts)
                if ts[-1] == TPS - 1:
                    dve.wait_ge(S["dchain"], nch[0])
                    if v >= 1:
                        dve.wait_ge(S["yr_r"], v)
                    for t in range(TPS):
                        ins = dve.bn_aggr(mvy[:, t, :], bs6[:, t, :])
                    ins.then_inc(S["yst"], 1)

            def first_residual(u, t):
                n = TPU * u + t
                x2 = xr[u % XS][:, t, :]
                dve.wait_ge(S["o1_mm"], n + 1)
                dve.wait_ge(S["xres_r"], n + 1)
                dve.tensor_tensor(x2, x2, PS[:, 2 + t, :], ALU.add).then_inc(S["x2_r"], 1)
                dve.wait_ge(S["x2_r"], n + 1)
                if u >= 1:
                    dve.wait_ge(S["x2st"], u)
                ins = dve.bn_stats(bx6[:, t, :], x2)
                if t < TPU - 1:
                    nch[0] += 1
                    ins.then_inc(S["dchain"], 1)
                    return
                chain(ins)
                if u >= 2:
                    dve.wait_ge(S["x2rs"], u - 1)
                for i in range(TPU):
                    ins = dve.bn_aggr(mvx[:, u % 2, i, :], bx6[:, i, :])
                ins.then_inc(S["x2st"], 1)

            def ffn(p, hs):
                g = gS[:, p % 2, :]
                for h in hs:
                    n = INNER * p + h
                    dve.wait_ge(S["relu_r"], n + 1)
                    if h == 0:
                        if p >= 2:
                            dve.wait_ge(S["o2_mm"], TPU * FP * (p - 1))
                        ins = dve.tensor_scalar(g, rr[:, 0, :], W2c[:, 0:1], b2c, ALU.mult, ALU.add)
                    else:
                        dve.wait_ge(S["ffn_r"], n)
                        ins = dve.scalar_tensor_tensor(out=g, in0=rr[:, h % RELU_RING, :], scalar=W2c[:, h:h + 1],
                                                       in1=g, op0=ALU.mult, op1=ALU.add)
                    ins.then_inc(S["ffn_r"], 1)

            def second_residual(u):
                for t in range(TPU):
                    n = TPU * u + t
                    x3 = xr[u % XS][:, t, :]
                    dve.wait_ge(S["o2_mm"], n + 1)
                    dve.wait_ge(S["xh2_r"], n + 1)
                    dve.tensor_tensor(x3, x3, PS[:, 6 + t, :], ALU.add).then_inc(S["x3_r"], 1)

            dve.wait_ge(S["y_ev"], NG)
            y_stats(0, range(TPS))
            y_stats(1, range(TPS))
            for u in range(NU + LAG):
                if u < NU:
                    first_residual(u, 0)
                if u >= LAG:
                    second_residual(u - LAG)
                v, h = u // 2 + 2, u % 2
                if v < NT:
                    y_stats(v, range(TPU * h, TPU * h + TPU))
                if u % 2 and 3 <= u <= NU + 1:
                    ffn((u - 3) // 2, H_B)
                if u < NU:
                    first_residual(u, 1)
                if u % 2 == 0 and 2 <= u <= NU:
                    ffn((u - 2) // 2, H_A)

        @block.tensor
        def _(pe):
            pe.wait_ge(S["ident_r"], 1)
            pe.wait_ge(S["ld_bc"], 32)
            pe.transpose(PS[:, 7, 0:128], bcn, ident[:, :]).then_inc(S["bct_mm"], 1)
            pe.wait_ge(S["crep_r"], 1)
            pe.wait_ge(S["bct_ev"], 1)

            def mod_row(i):
                j = MOD_ORDER[i]
                if i < 2:
                    pe.wait_ge(ld_wm[j], 16)
                else:
                    pe.wait_ge(ld_wm[j], 16)
                    pe.wait_ge(S["mod_ev"], i)
                for k in range(QB):
                    w = wm_first[:, i, k, :] if i < 2 else wm_later[:, k, :]
                    mm = pe.matmul(PS[:, 6 + i % 2, :], crep[:, k, :], w, start=(k == 0), stop=(k == QB - 1))
                mm.then_inc(S["mod_mm"], 1)

            mod_row(0)
            mod_row(1)

            for half in range(HALVES):
                base = half * HSTEPS
                pe.wait_ge(S["v0_r"], 2 * (half + 1))
                if half:
                    pe.wait_ge(S["y_ev"], half * HG)
                for n in range(STEPS):
                    k, o, r, w = n // OCT, n % OCT, (base + n) % 2, 2 ** (n // OCT)
                    b = (base + n) % BDR
                    pe.wait_ge(S["bdt_r"], base + n + 1)
                    if base + n >= 2:
                        pe.wait_ge(S["lvl_ev"], base + n - 1)
                    for j in range(8):
                        g = 8 * o + j
                        for e in QD:
                            pe.matmul(pv_ps(r)[e:e + 32, j, 0:w + NS], BDTs[e:e + 32, b, j, :], PV[e:e + 32, g, PW - w:PW + NS],
                                      start=True, stop=True)
                        for e in QD:
                            mm = pe.matmul(w_ps(r)[e:e + 32, j, 0:w], BDs[e:e + 32, b, j, :], WP[e:e + 32, g, L + 1 - w:L + 1],
                                           start=True, stop=True)
                    mm.then_inc(S["lvl_mm"], 1)
                pe.wait_ge(S["lvl_ev"], base + STEPS)
                pe.wait_ge(S["cm_r"], 4 * (half + 1))
                for b in range(2):
                    for m in range(4):
                        for e in range(4):
                            g = (4 * b + e) * 4 + m
                            mm = pe.matmul(PS[32 * e:32 * e + 32, 4, b * P:(b + 1) * P], CM[:, g, :], PV[:, g, 0:L],
                                           start=(m == 0), stop=(m == 3))
                mm.then_inc(S["k_mm"], 1)
                pe.wait_ge(S["bdt_r"], base + STEPS + OCT)
                for g in range(HG):
                    for e in QD:
                        mm = pe.matmul(PS[e:e + 32, 5, g:g + 1], BDs[e:e + 32, (base + STEPS + g // 8) % BDR, g % 8, :],
                                       WP[e:e + 32, g, L:L + 1], start=True, stop=True)
                mm.then_inc(S["w128_mm"], 1)

                def input_mats(q):
                    n = 8 * half + q
                    if q >= 2:
                        pe.wait_ge(S["ut_ev"], n - 1)
                    for i in range(4):
                        mm = pe.transpose(PS[:, 6 + q % 2, i * P:(i + 1) * P], PV[:, 4 * q + i, 0:L], ident[:, :])
                    mm.then_inc(S["ut_mm"], 1)

                if half == 0:
                    pe.wait_ge(S["xy_r"], NC)
                input_mats(0)
                for q in range(8):
                    n = 8 * half + q
                    if q < 7:
                        input_mats(q + 1)
                    pe.wait_ge(S["ut_ev"], n + 1)
                    if q >= 4:
                        pe.wait_ge(S["u_ev"], n - 3)
                    for i in range(4):
                        for e in range(4):
                            d = (half * HG + 4 * q + i) * GC + 2 * e
                            mm = pe.matmul(PS[32 * e:32 * e + 32, q % 4, i * P:(i + 1) * P],
                                           Uring[:, q % 2, i * P + 32 * e:i * P + 32 * e + 32], XY[:, d:d + 2, :],
                                           start=True, stop=True)
                    mm.then_inc(S["u_mm"], 1)
                pe.wait_ge(S["u_ev"], 8 * half + 6)
                for i in range(SSTEPS):
                    k, o, n = i // OCT, i % OCT, base + STEPS + i
                    pe.wait_ge(S["bdf_r"], half * SSTEPS + i + 1)
                    if i == 1:
                        pe.wait_ge(S["u_ev"], 8 * (half + 1))
                    if i >= 2:
                        pe.wait_ge(S["scan_h"], half * SSTEPS + i - 1)
                    for j in range(8):
                        g = 8 * o + j
                        mm = pe.matmul(pv_ps(n % 2)[:, j, 0:NS + NC], BDF[:, n % 2, j, :], PV[:, g, H0:PW + NS], start=True, stop=True)
                    mm.then_inc(S["lvl_mm"], 1)
                pe.wait_ge(S["scan_h"], (half + 1) * SSTEPS)
                pe.wait_ge(S["w128_ev"], half + 1)
                for g in range(HG):
                    n = half * HG + g
                    if half == 0 and g % MODE == 0 and 2 <= g // MODE < 6:
                        mod_row(g // MODE)
                    if half == HALVES - 1 and 6 <= g < 6 + QB:
                        q = g - 6
                        pe.wait_ge(S["ld_wo"], 16)
                        if q >= 2:
                            pe.wait_ge(S["wo_ev"], q - 1)
                        for o in range(QB):
                            mm = pe.transpose(PS[:, 6 + q % 2, o * P:(o + 1) * P], WoN[:, o, q * P:(q + 1) * P], ident[:, :])
                        mm.then_inc(S["wo_tr"], 1)
                    if half == HALVES - 1 and g == 18:
                        pe.wait_ge(S["ld_w"], 16 * 15)
                        for r in range(2):
                            for q in range(QB):
                                mm = pe.matmul(PS[64 * r:64 * r + 64, 5, 0:1], WinS[:, q, :], cbsb[:, 4 + q:5 + q], start=(q == 0), stop=(q == QB - 1))
                        mm.then_inc(S["prep_mm"], 1)
                    if g >= 4:
                        pe.wait_ge(S["y_ev"], n - 3)
                    pe.wait_ge(S["bdh_r"], n + 1)
                    if g == 0:
                        pe.wait_ge(S["bz_r"], half + 1)
                    pe.matmul(PS[:, g % 4, :], WP[:, g, 0:L], BDH[:, g % 2, :, :], start=True, stop=False,
                              skip_group_check=True).then_inc(S["o_mm"], 1)
                    pe.wait_ge(t_ld[n % 3], 16 * (n // 3 + 1))
                    for h in range(GC):
                        for a in range(0, P, 64):
                            mm = pe.matmul(PS[a:a + 64, g % 4, h * NC:(h + 1) * NC], Tring[:, n % 3, h, a:a + 64], XY[:, n * GC + h, :],
                                           start=False, stop=(h == GC - 1), skip_group_check=True)
                    mm.then_inc(S["t_mm"], 1)

            pe.wait_ge(S["wo_ev"], QB)
            pe.wait_ge(S["y_ev"], NG)
            pe.wait_ge(S["prep_r"], 2)

            def t_y(u, b):
                pe.wait_ge(S["yh_r"], TPU * (u + 1))
                if u >= 1:
                    pe.wait_ge(S["gelu_r"], QB * (u - 1) + 2 * (b + 1))
                for q in (2 * b, 2 * b + 1):
                    for t in range(TPU):
                        i = (q % 2) * UW + t * P
                        mm = pe.transpose(PS[:, b, i:i + P], hatY[:, t, q * P:(q + 1) * P], ident[:, :])
                mm.then_inc(S["ty_mm"], 1)

            def out1(u, t, qs):
                n = TPU * u + t
                if qs[0] == 0:
                    pe.wait_ge(S["gelu_r"], QB * (u + 1))
                    if u >= 1:
                        pe.wait_ge(S["x2_r"], n - TPU + 1)
                for q in qs:
                    pe.matmul(PS[:, 2 + t, :], zT[:, u % 2, q, t * P:(t + 1) * P], WoT[:, q, :], start=(q == 0), stop=False)
                if qs[-1] == QB - 1:
                    pe.matmul(PS[:, 2 + t, :], ones_bf[0:3, :], bias1[0:3, :], start=False, stop=True).then_inc(S["o1_mm"], 1)

            def t_x(u, b):
                pe.wait_ge(S["xh2_r"], TPU * (u + 1))
                if 2 * u + b >= 1:
                    pe.wait_ge(S["xT_r"], 2 * u + b)
                for q in (2 * b, 2 * b + 1):
                    for t in range(TPU):
                        i = (q % 2) * UW + t * P
                        mm = pe.transpose(PS[:, 4, i:i + P], hatX[:, t, q * P:(q + 1) * P], ident[:, :])
                mm.then_inc(S["tx_mm"], 1)

            def s_prod(u):
                pe.wait_ge(S["xT_r"], 2 * (u + 1))
                if u >= FP:
                    pe.wait_ge(S["relu_r"], INNER * (u // FP))
                for q in range(QB):
                    for a in range(2):
                        x = x2T[:, q, :].rearrange("p (t a i) -> p a t i", a=2, i=M)[:, a, :, :]
                        mm = pe.matmul(PS[M * a:M * a + M, 5, (u % FP) * P:(u % FP + 1) * P], WinS[:, q, :], x,
                                       start=(q == 0), stop=(q == QB - 1))
                mm.then_inc(S["s_mm"], 1)

            def out2(u):
                pe.wait_ge(S["ffn_r"], INNER * (u // FP + 1))
                if u >= 1:
                    pe.wait_ge(S["x3_r"], TPU * u)
                for t in range(TPU):
                    i = (u % FP) * P + t * M
                    for a in range(2):
                        pe.matmul(PS[M * a:M * a + M, 6 + t, :], gS[M * a:M * a + M, (u // FP) % 2, i:i + M], WoutS[M * a:M * a + M, :],
                                  start=True, stop=False)
                for t in range(TPU):
                    pe.matmul(PS[:, 6 + t, :], ones_bf[0:3, :], bias2[0:3, :], start=False, stop=True).then_inc(S["o2_mm"], 1)

            t_y(0, 0)
            t_y(0, 1)
            for u in range(NU + LAG):
                if u < NU:
                    out1(u, 0, (0, 1, 2, 3))
                if u % 2 == 0 and 2 <= u <= NU:
                    s_prod(u - 2)
                if u >= LAG:
                    out2(u - LAG)
                if u + 1 < NU:
                    t_y(u + 1, 0)
                    t_y(u + 1, 1)
                if u % 2 == 0 and 2 <= u <= NU:
                    t_x(u - 1, 0)
                if u < NU:
                    out1(u, 1, (0, 1))
                if 1 <= u <= NU:
                    t_x(u - 1, 1 - u % 2)
                if u < NU:
                    out1(u, 1, (2, 3))
                if u % 2 and u <= NU:
                    t_x(u - 1, 1)
                if u % 2 == 0 and 2 <= u <= NU:
                    s_prod(u - 1)


def scan_add(dve, S, PV, pv_ps, half, base, i, ALU):
    k, o, n = i // OCT, i % OCT, base + STEPS + i
    w = 2 ** k
    dve.wait_ge(S["lvl_ev"], n + 1)
    st = PV[:, 8 * o:8 * o + 8, H0 + w:H0 + NC]
    dve.tensor_tensor(st, st, pv_ps(n % 2)[:, :, 0:NC - w], ALU.add).then_inc(S["scan_h"], 1)


_INS = ['L0_attn_x', 'L0_attn_A', 'L0_attn_Bm', 'L0_attn_Cm', 'L0_attn_Dm', 'L0_attn_ln_w', 'L0_attn_ln_b',
        'L0_attn_W_out', 'L0_attn_b_out', 'L0_ffn_Win', 'L0_ffn_bin_', 'L0_ffn_W1', 'L0_ffn_b1', 'L0_ffn_W2',
        'L0_ffn_b2', 'L0_ffn_Wout', 'L0_ffn_bout', 'L0_c', 'L0_wmod']


def kernel(**inputs):
    import numpy as _np
    import concourse.bacc as _bacc
    from concourse import mybir as _mybir
    from concourse.bass_utils import run_bass_kernel_spmd as _run

    nc = _bacc.Bacc("TRN2", target_bir_lowering=False, num_devices=1)
    arrays, args = {}, []
    for name in _INS:
        a = _np.ascontiguousarray(inputs[name])
        arrays[f"in_{name}"] = a
        args.append(nc.dram_tensor(f"in_{name}", a.shape, _mybir.dt.from_np(a.dtype), kind="ExternalInput").ap())
    res = nc.dram_tensor("out_0", (1, T, D), _mybir.dt.float32, kind="ExternalOutput").ap()
    adaln_ssm_kernel(nc, *args, res)
    r = _run(nc, [arrays], core_ids=[0])
    return r.results[0]["out_0"]
```
